# Optimizing a Trainium2 kernel written in Bass

```python
import numpy as np
import jax
import jax.numpy as jnp

def _softmax(x, axis=-1):
    return jax.nn.softmax(x, axis=axis)

def _gelu(x):
    return jax.nn.gelu(x, approximate=True)

def _silu(x):
    return jax.nn.silu(x)

def _sigmoid(x):
    return jax.nn.sigmoid(x)

def _layernorm(x, axis=-1, eps=1e-05):
    m = jnp.mean(x, axis=axis, keepdims=True)
    v = jnp.var(x, axis=axis, keepdims=True)
    return (x - m) / jnp.sqrt(v + eps)

def _scatter_add(tgt, idx, src, axis=0):
    return tgt.at[idx].add(src)

def _segment_sum(src, seg, n):
    return jax.ops.segment_sum(src, seg, n)
kernel_name = 'mk_xattn_seq_d4_seqx_r8_e338f8'

def setup_inputs(seed: int=0):
    np.random.seed(seed)
    _w = jnp.asarray

    def _rec_inputs():
        import jax
        import jax.numpy as jnp
        _rk = jax.random.key(seed)
        x = -0.0002928 + 1 * jax.random.normal(jax.random.fold_in(_rk, 1), (64, 128, 128), jnp.float32)
        _lenS = 128 - jax.random.randint(jax.random.fold_in(_rk, 7), (64,), 0, max(1, 128 // 4) + 1, jnp.int32)
        _lenS2 = 77 - jax.random.randint(jax.random.fold_in(_rk, 8), (64,), 0, max(1, 77 // 4) + 1, jnp.int32)
        _ctx_1024P = jax.random.normal(jax.random.fold_in(_rk, 11), (64, 16, 128), jnp.float32)
        _ctx_1024c = jax.random.dirichlet(jax.random.fold_in(_rk, 511), 0.3 * jnp.ones((16,), jnp.float32), (64, 77))
        _ctx_1024t = jnp.einsum('bsk,bkd->bsd', _ctx_1024c, _ctx_1024P)
        _ctx_1024t = _ctx_1024t * jax.lax.rsqrt(jnp.mean(jnp.square(_ctx_1024t)) + 1e-12) * 0.953939
        ctx_1024 = -1.39393e-06 + 0.999914 * (_ctx_1024t + 0.3 * jax.random.normal(jax.random.fold_in(_rk, 611), (64, 77, 128), jnp.float32))
        _validS = jnp.arange(128)[None, :] < _lenS[:, None]
        _validS2 = jnp.arange(77)[None, :] < _lenS2[:, None]
        _causal = jnp.tril(jnp.ones((128, 128), dtype=bool))
        mask_1xS2_bf0 = jnp.logical_not(jnp.ones((1, 77), dtype=bool))
        mask_BxSxS2_ik1 = jnp.where(jnp.broadcast_to(_validS2[:, None, :], (64, 128, 77)), 1, 0).astype(jnp.int32)
        return (x, ctx_1024, mask_1xS2_bf0, mask_BxSxS2_ik1)
    x, ctx_1024, mask_1xS2_bf0, mask_BxSxS2_ik1 = _rec_inputs()

    def _L0_xattn_setup():
        import jax, jax.numpy as jnp
        import numpy as np
        B, LX, LY = (2, 256, 256)
        E, H = (128, 16)
        HD = E // H
        FF = 512
        EPS = 1e-05

        def _rope_tables(L, d):
            inv = 1.0 / 10000.0 ** (jnp.arange(0, d, 2, dtype=jnp.float32) / d)
            t = jnp.arange(L, dtype=jnp.float32)
            f = jnp.outer(t, inv)
            return (jnp.cos(f), jnp.sin(f))

        def _apply_rope(x, cos, sin):
            d2 = x.shape[-1] // 2
            x1, x2 = (x[..., :d2], x[..., d2:])
            c = cos[None, :, None, :]
            s = sin[None, :, None, :]
            return jnp.concatenate([x1 * c - x2 * s, x2 * c + x1 * s], axis=-1)

        def _ln(x, g, b):
            m = jnp.mean(x, axis=-1, keepdims=True)
            v = jnp.var(x, axis=-1, keepdims=True)
            return (x - m) / jnp.sqrt(v + EPS) * g + b

        def _attn(q, k, v, causal):
            s = jnp.einsum('blhd,bmhd->bhlm', q, k)
            if causal:
                Lq, Lk = (s.shape[2], s.shape[3])
                mask = jnp.tril(jnp.ones((Lq, Lk), dtype=bool))
                s = jnp.where(mask, s, -jnp.inf)
            p = jax.nn.softmax(s, axis=-1)
            return jnp.einsum('bhlm,bmhd->blhd', p, v)

        def _forward(x, y, ln1_g, ln1_b, sa_wq, sa_bq, sa_wk, sa_bk, sa_wv, sa_bv, sa_wo, sa_bo, ln2_g, ln2_b, ca_wq, ca_bq, ca_wk, ca_bk, ca_wv, ca_bv, ca_wo, ca_bo, ln3_g, ln3_b, fc1_w, fc1_b, fc2_w, fc2_b):
            Bx, Lx, _ = x.shape
            Ly = y.shape[1]
            cos, sin = _rope_tables(max(Lx, Ly), HD)
            scale = HD ** (-0.5)
            h = _ln(x, ln1_g, ln1_b)
            q = (h @ sa_wq + sa_bq).reshape(Bx, Lx, H, HD) * scale
            k = (h @ sa_wk + sa_bk).reshape(Bx, Lx, H, HD)
            v = (h @ sa_wv + sa_bv).reshape(Bx, Lx, H, HD)
            q = _apply_rope(q, cos[:Lx], sin[:Lx])
            k = _apply_rope(k, cos[:Lx], sin[:Lx])
            a = _attn(q, k, v, causal=True).reshape(Bx, Lx, E)
            x = x + (a @ sa_wo + sa_bo)
            h = _ln(x, ln2_g, ln2_b)
            q = (h @ ca_wq + ca_bq).reshape(Bx, Lx, H, HD) * scale
            k = (y @ ca_wk + ca_bk).reshape(Bx, Ly, H, HD)
            v = (y @ ca_wv + ca_bv).reshape(Bx, Ly, H, HD)
            q = _apply_rope(q, cos[:Lx], sin[:Lx])
            k = _apply_rope(k, cos[:Ly], sin[:Ly])
            a = _attn(q, k, v, causal=False).reshape(Bx, Lx, E)
            x = x + (a @ ca_wo + ca_bo)
            h = _ln(x, ln3_g, ln3_b)
            return x + (jax.nn.gelu(h @ fc1_w + fc1_b) @ fc2_w + fc2_b)
        key = jax.random.key(seed)
        ks = jax.random.split(key, 16)

        def w(k, *s):
            return jax.random.normal(k, s, jnp.float32) * 0.02
        z = lambda *s: jnp.zeros(s, jnp.float32)
        o = lambda *s: jnp.ones(s, jnp.float32)
        return {'x': jax.random.normal(ks[0], (B, LX, E), jnp.float32), 'y': jax.random.normal(ks[1], (B, LY, E), jnp.float32), 'ln1_g': o(E), 'ln1_b': z(E), 'sa_wq': w(ks[2], E, E), 'sa_bq': z(E), 'sa_wk': w(ks[3], E, E), 'sa_bk': z(E), 'sa_wv': w(ks[4], E, E), 'sa_bv': z(E), 'sa_wo': w(ks[5], E, E), 'sa_bo': z(E), 'ln2_g': o(E), 'ln2_b': z(E), 'ca_wq': w(ks[6], E, E), 'ca_bq': z(E), 'ca_wk': w(ks[7], E, E), 'ca_bk': z(E), 'ca_wv': w(ks[8], E, E), 'ca_bv': z(E), 'ca_wo': w(ks[9], E, E), 'ca_bo': z(E), 'ln3_g': o(E), 'ln3_b': z(E), 'fc1_w': w(ks[10], E, FF), 'fc1_b': z(FF), 'fc2_w': w(ks[11], FF, E), 'fc2_b': z(E)}
    _L0_xattn_all = _L0_xattn_setup()
    _L0_xattn_in = {k: v for k, v in _L0_xattn_all.items() if k in ('ln1_g', 'ln1_b', 'sa_wq', 'sa_bq', 'sa_wk', 'sa_bk', 'sa_wv', 'sa_bv', 'sa_wo', 'sa_bo', 'ln2_g', 'ln2_b', 'ca_wq', 'ca_bq', 'ca_wk', 'ca_bk', 'ca_wv', 'ca_bv', 'ca_wo', 'ca_bo', 'ln3_g', 'ln3_b', 'fc1_w', 'fc1_b', 'fc2_w', 'fc2_b')}
    del _L0_xattn_all

    def _L1_xattn_setup():
        import jax, jax.numpy as jnp
        import numpy as np
        D, H, E, K, DFF = (128, 16, 8, 2, 512)
        B, L, T = (4, 64, 256)
        EPS = 1e-05

        def _xavier(key, shape):
            fan_in, fan_out = (shape[-1], shape[-2])
            a = jnp.sqrt(6.0 / (fan_in + fan_out))
            return jax.random.uniform(key, shape, jnp.float32, -a, a)

        def _ln(x, g, b):
            m = x.mean(-1, keepdims=True)
            v = ((x - m) ** 2).mean(-1, keepdims=True)
            return (x - m) / jnp.sqrt(v + EPS) * g + b

        def _mha(q_in, kv_in, in_w, in_b, out_w, out_b):
            wq, wk, wv = jnp.split(in_w, 3, axis=0)
            bq, bk, bv = jnp.split(in_b, 3, axis=0)
            dh = D // H

            def heads(x, w, b):
                y = x @ w.T + b
                return y.reshape(x.shape[0], x.shape[1], H, dh).transpose(0, 2, 1, 3)
            q = heads(q_in, wq, bq)
            k = heads(kv_in, wk, bk)
            v = heads(kv_in, wv, bv)
            scores = jnp.einsum('bhqd,bhkd->bhqk', q, k) / jnp.sqrt(jnp.float32(dh))
            attn = jax.nn.softmax(scores, axis=-1)
            out = jnp.einsum('bhqk,bhkd->bhqd', attn, v)
            out = out.transpose(0, 2, 1, 3).reshape(q_in.shape[0], q_in.shape[1], D)
            return out @ out_w.T + out_b

        def _fuse_moe(x, ln_g, ln_b, rw, rb, fc1_w, fc1_b, fc2_w, fc2_b):
            h = _ln(x, ln_g, ln_b)
            logits = h @ rw.T + rb
            vals, idx = jax.lax.top_k(logits, K)
            gates = jax.nn.softmax(vals, axis=-1)
            N = x.shape[0] * x.shape[1]
            hf = h.reshape(N, D)
            h1 = jax.nn.gelu(jnp.einsum('nd,efd->enf', hf, fc1_w) + fc1_b[:, None, :], approximate=False)
            eo = jnp.einsum('enf,edf->end', h1, fc2_w) + fc2_b[:, None, :]
            idx_f = idx.reshape(N, K)
            gates_f = gates.reshape(N, K)
            gathered = eo[idx_f, jnp.arange(N)[:, None], :]
            mixed = (gathered * gates_f[..., None]).sum(axis=1).reshape(x.shape)
            return x + mixed
        key = jax.random.key(seed)
        ks = jax.random.split(key, 16)
        inp = {'latents': jax.random.normal(ks[0], (B, L, D), jnp.float32), 'tokens': jax.random.normal(ks[1], (B, T, D), jnp.float32), 'sa_ln_g': jnp.ones((D,)), 'sa_ln_b': jnp.zeros((D,)), 'sa_in_w': _xavier(ks[2], (3 * D, D)), 'sa_in_b': jnp.zeros((3 * D,)), 'sa_out_w': _xavier(ks[3], (D, D)), 'sa_out_b': jnp.zeros((D,)), 'ca_q_ln_g': jnp.ones((D,)), 'ca_q_ln_b': jnp.zeros((D,)), 'ca_kv_ln_g': jnp.ones((D,)), 'ca_kv_ln_b': jnp.zeros((D,)), 'ca_in_w': _xavier(ks[4], (3 * D, D)), 'ca_in_b': jnp.zeros((3 * D,)), 'ca_out_w': _xavier(ks[5], (D, D)), 'ca_out_b': jnp.zeros((D,)), 'moe_ln_g': jnp.ones((D,)), 'moe_ln_b': jnp.zeros((D,)), 'router_w': _xavier(ks[6], (E, D)), 'router_b': jnp.zeros((E,)), 'e_fc1_w': jax.vmap(lambda k: _xavier(k, (DFF, D)))(jax.random.split(ks[7], E)), 'e_fc1_b': jnp.zeros((E, DFF)), 'e_fc2_w': jax.vmap(lambda k: _xavier(k, (D, DFF)))(jax.random.split(ks[8], E)), 'e_fc2_b': jnp.zeros((E, D))}
        return inp
    _L1_xattn_all = _L1_xattn_setup()
    _L1_xattn_in = {k: v for k, v in _L1_xattn_all.items() if k in ('sa_ln_g', 'sa_ln_b', 'sa_in_w', 'sa_in_b', 'sa_out_w', 'sa_out_b', 'ca_q_ln_g', 'ca_q_ln_b', 'ca_kv_ln_g', 'ca_kv_ln_b', 'ca_in_w', 'ca_in_b', 'ca_out_w', 'ca_out_b', 'moe_ln_g', 'moe_ln_b', 'router_w', 'router_b', 'e_fc1_w', 'e_fc1_b', 'e_fc2_w', 'e_fc2_b')}
    del _L1_xattn_all

    def _L2_xattn_setup():
        import jax, jax.numpy as jnp
        import numpy as np
        D = 128
        D_STATE = 128
        N_HEADS = 8
        D_INNER = 2 * D
        HEADDIM = 64
        H_M = D_INNER // HEADDIM
        D_CONV = 4
        CONV_DIM = D_INNER + 2 * D_STATE
        D_IN_PROJ = 2 * D_INNER + 2 * D_STATE + H_M
        B = 1
        LQ = 128
        LK = 256
        EPS = 1e-05

        def _rms(x, w):
            return x * jax.lax.rsqrt(jnp.mean(x * x, axis=-1, keepdims=True) + EPS) * w

        def _ln(x, w, b):
            mu = jnp.mean(x, axis=-1, keepdims=True)
            v = jnp.mean((x - mu) ** 2, axis=-1, keepdims=True)
            return (x - mu) * jax.lax.rsqrt(v + EPS) * w + b

        def _mamba2_block(x, norm_w, in_proj_w, conv_w, conv_b, dt_bias, A_log, D_skip, gnorm_w, out_proj_w):
            b, L, _ = x.shape
            resid = x
            zxbcdt = _rms(x, norm_w) @ in_proj_w
            z = zxbcdt[..., :D_INNER]
            xBC = zxbcdt[..., D_INNER:D_INNER + CONV_DIM]
            dt = jax.nn.softplus(zxbcdt[..., -H_M:] + dt_bias)
            padded = jnp.pad(xBC, ((0, 0), (D_CONV - 1, 0), (0, 0)))
            conv = conv_b + sum((padded[:, k:k + L, :] * conv_w[:, k] for k in range(D_CONV)))
            xBC = jax.nn.silu(conv)
            xh = xBC[..., :D_INNER].reshape(b, L, H_M, HEADDIM)
            Bm = xBC[..., D_INNER:D_INNER + D_STATE]
            Cm = xBC[..., D_INNER + D_STATE:]
            A = -jnp.exp(A_log)
            decay = jnp.exp(dt * A)
            dbx = dt[..., None] * xh

            def step(h, inp):
                dec, u, bt, ct = inp
                h = h * dec[:, :, None, None] + u[..., None] * bt[:, None, None, :]
                y = jnp.einsum('bhpn,bn->bhp', h, ct)
                return (h, y)
            h0 = jnp.zeros((b, H_M, HEADDIM, D_STATE), x.dtype)
            xs = (decay.transpose(1, 0, 2), dbx.transpose(1, 0, 2, 3), Bm.transpose(1, 0, 2), Cm.transpose(1, 0, 2))
            _, ys = jax.lax.scan(step, h0, xs)
            y = ys.transpose(1, 0, 2, 3) + D_skip[None, None, :, None] * xh
            u = _rms(y.reshape(b, L, D_INNER) * jax.nn.silu(z), gnorm_w)
            return resid + u @ out_proj_w

        def _cross_attention(x, enc, pad_mask, ln_w, ln_b, Wq, Wk, Wv, Wo):
            b, Lq, _ = x.shape
            Lk = enc.shape[1]
            dh = D // N_HEADS
            resid = x
            xn = _ln(x, ln_w, ln_b)
            q = (xn @ Wq).reshape(b, Lq, N_HEADS, dh)
            k = (enc @ Wk).reshape(b, Lk, N_HEADS, dh)
            v = (enc @ Wv).reshape(b, Lk, N_HEADS, dh)
            scores = jnp.einsum('bqhd,bkhd->bhqk', q, k) * np.float32(1.0 / np.sqrt(dh))
            scores = jnp.where(pad_mask[:, None, None, :], jnp.float32(-1000000000.0), scores)
            p = jax.nn.softmax(scores, axis=-1)
            ctx = jnp.einsum('bhqk,bkhd->bqhd', p, v).reshape(b, Lq, D)
            return resid + ctx @ Wo
        key = jax.random.key(seed)
        ks = jax.random.split(key, 10)
        s = 0.02
        return {'x': jax.random.normal(ks[0], (B, LQ, D), jnp.float32), 'encoder_out': jax.random.normal(ks[1], (B, LK, D), jnp.float32), 'encoder_padding_mask': jnp.zeros((B, LK), dtype=bool), 'm_norm_w': jnp.ones((D,), jnp.float32), 'in_proj_w': s * jax.random.normal(ks[2], (D, D_IN_PROJ), jnp.float32), 'conv_w': s * jax.random.normal(ks[3], (CONV_DIM, D_CONV), jnp.float32), 'conv_b': jnp.zeros((CONV_DIM,), jnp.float32), 'dt_bias': jnp.full((H_M,), float(np.log(np.expm1(0.01))), jnp.float32), 'A_log': jnp.log(jnp.linspace(1.0, 16.0, H_M)).astype(jnp.float32), 'D_skip': jnp.ones((H_M,), jnp.float32), 'gnorm_w': jnp.ones((D_INNER,), jnp.float32), 'out_proj_w': s * jax.random.normal(ks[4], (D_INNER, D), jnp.float32), 'ca_ln_w': jnp.ones((D,), jnp.float32), 'ca_ln_b': jnp.zeros((D,), jnp.float32), 'Wq': s * jax.random.normal(ks[5], (D, D), jnp.float32), 'Wk': s * jax.random.normal(ks[6], (D, D), jnp.float32), 'Wv': s * jax.random.normal(ks[7], (D, D), jnp.float32), 'Wo': s * jax.random.normal(ks[8], (D, D), jnp.float32)}
    _L2_xattn_all = _L2_xattn_setup()
    _L2_xattn_in = {k: v for k, v in _L2_xattn_all.items() if k in ('m_norm_w', 'in_proj_w', 'conv_w', 'conv_b', 'dt_bias', 'A_log', 'D_skip', 'gnorm_w', 'out_proj_w', 'ca_ln_w', 'ca_ln_b', 'Wq', 'Wk', 'Wv', 'Wo')}
    del _L2_xattn_all

    def _L3_xattn_setup():
        import jax, jax.numpy as jnp
        import numpy as np
        H = 128
        NH = 16
        HD = H // NH
        EPS = 1e-05

        def _split_heads(x, B, L):
            return x.reshape(B, L, NH, HD).transpose(0, 2, 1, 3)
        key = jax.random.key(seed)
        ks = jax.random.split(key, 16)
        B, LQ, LK = (2, 128, 256)
        s = 1.0 / np.sqrt(H)
        inp = {'query': jax.random.normal(ks[0], (B, LQ, H), jnp.float32), 'key': jax.random.normal(ks[1], (B, LK, H), jnp.float32), 'value': jax.random.normal(ks[2], (B, LK, H), jnp.float32), 'mask': jax.random.randint(ks[3], (B, LQ, LK), 0, 2, jnp.int32), 'Wq': jax.random.normal(ks[4], (H, H), jnp.float32) * s, 'bq': jnp.zeros((H,), jnp.float32), 'Wk': jax.random.normal(ks[5], (H, H), jnp.float32) * s, 'bk': jnp.zeros((H,), jnp.float32), 'Wv': jax.random.normal(ks[6], (H, H), jnp.float32) * s, 'bv': jnp.zeros((H,), jnp.float32), 'Wo': jax.random.normal(ks[7], (H, H), jnp.float32) * s, 'bo': jnp.zeros((H,), jnp.float32), 'ln_g': jnp.ones((H,), jnp.float32), 'ln_b': jnp.zeros((H,), jnp.float32)}
        return inp
    _L3_xattn_all = _L3_xattn_setup()
    _L3_xattn_in = {k: v for k, v in _L3_xattn_all.items() if k in ('Wq', 'bq', 'Wk', 'bk', 'Wv', 'bv', 'Wo', 'bo', 'ln_g', 'ln_b')}
    del _L3_xattn_all
    return {'x': x, 'ctx_1024': ctx_1024, 'mask_1xS2_bf0': mask_1xS2_bf0, 'mask_BxSxS2_ik1': mask_BxSxS2_ik1, 'L0_xattn_ln1_g': _L0_xattn_in['ln1_g'], 'L0_xattn_ln1_b': _L0_xattn_in['ln1_b'], 'L0_xattn_sa_wq': _L0_xattn_in['sa_wq'], 'L0_xattn_sa_bq': _L0_xattn_in['sa_bq'], 'L0_xattn_sa_wk': _L0_xattn_in['sa_wk'], 'L0_xattn_sa_bk': _L0_xattn_in['sa_bk'], 'L0_xattn_sa_wv': _L0_xattn_in['sa_wv'], 'L0_xattn_sa_bv': _L0_xattn_in['sa_bv'], 'L0_xattn_sa_wo': _L0_xattn_in['sa_wo'], 'L0_xattn_sa_bo': _L0_xattn_in['sa_bo'], 'L0_xattn_ln2_g': _L0_xattn_in['ln2_g'], 'L0_xattn_ln2_b': _L0_xattn_in['ln2_b'], 'L0_xattn_ca_wq': _L0_xattn_in['ca_wq'], 'L0_xattn_ca_bq': _L0_xattn_in['ca_bq'], 'L0_xattn_ca_wk': _L0_xattn_in['ca_wk'], 'L0_xattn_ca_bk': _L0_xattn_in['ca_bk'], 'L0_xattn_ca_wv': _L0_xattn_in['ca_wv'], 'L0_xattn_ca_bv': _L0_xattn_in['ca_bv'], 'L0_xattn_ca_wo': _L0_xattn_in['ca_wo'], 'L0_xattn_ca_bo': _L0_xattn_in['ca_bo'], 'L0_xattn_ln3_g': _L0_xattn_in['ln3_g'], 'L0_xattn_ln3_b': _L0_xattn_in['ln3_b'], 'L0_xattn_fc1_w': _L0_xattn_in['fc1_w'], 'L0_xattn_fc1_b': _L0_xattn_in['fc1_b'], 'L0_xattn_fc2_w': _L0_xattn_in['fc2_w'], 'L0_xattn_fc2_b': _L0_xattn_in['fc2_b'], 'L1_xattn_sa_ln_g': _L1_xattn_in['sa_ln_g'], 'L1_xattn_sa_ln_b': _L1_xattn_in['sa_ln_b'], 'L1_xattn_sa_in_w': _L1_xattn_in['sa_in_w'], 'L1_xattn_sa_in_b': _L1_xattn_in['sa_in_b'], 'L1_xattn_sa_out_w': _L1_xattn_in['sa_out_w'], 'L1_xattn_sa_out_b': _L1_xattn_in['sa_out_b'], 'L1_xattn_ca_q_ln_g': _L1_xattn_in['ca_q_ln_g'], 'L1_xattn_ca_q_ln_b': _L1_xattn_in['ca_q_ln_b'], 'L1_xattn_ca_kv_ln_g': _L1_xattn_in['ca_kv_ln_g'], 'L1_xattn_ca_kv_ln_b': _L1_xattn_in['ca_kv_ln_b'], 'L1_xattn_ca_in_w': _L1_xattn_in['ca_in_w'], 'L1_xattn_ca_in_b': _L1_xattn_in['ca_in_b'], 'L1_xattn_ca_out_w': _L1_xattn_in['ca_out_w'], 'L1_xattn_ca_out_b': _L1_xattn_in['ca_out_b'], 'L1_xattn_moe_ln_g': _L1_xattn_in['moe_ln_g'], 'L1_xattn_moe_ln_b': _L1_xattn_in['moe_ln_b'], 'L1_xattn_router_w': _L1_xattn_in['router_w'], 'L1_xattn_router_b': _L1_xattn_in['router_b'], 'L1_xattn_e_fc1_w': _L1_xattn_in['e_fc1_w'], 'L1_xattn_e_fc1_b': _L1_xattn_in['e_fc1_b'], 'L1_xattn_e_fc2_w': _L1_xattn_in['e_fc2_w'], 'L1_xattn_e_fc2_b': _L1_xattn_in['e_fc2_b'], 'L2_xattn_m_norm_w': _L2_xattn_in['m_norm_w'], 'L2_xattn_in_proj_w': _L2_xattn_in['in_proj_w'], 'L2_xattn_conv_w': _L2_xattn_in['conv_w'], 'L2_xattn_conv_b': _L2_xattn_in['conv_b'], 'L2_xattn_dt_bias': _L2_xattn_in['dt_bias'], 'L2_xattn_A_log': _L2_xattn_in['A_log'], 'L2_xattn_D_skip': _L2_xattn_in['D_skip'], 'L2_xattn_gnorm_w': _L2_xattn_in['gnorm_w'], 'L2_xattn_out_proj_w': _L2_xattn_in['out_proj_w'], 'L2_xattn_ca_ln_w': _L2_xattn_in['ca_ln_w'], 'L2_xattn_ca_ln_b': _L2_xattn_in['ca_ln_b'], 'L2_xattn_Wq': _L2_xattn_in['Wq'], 'L2_xattn_Wk': _L2_xattn_in['Wk'], 'L2_xattn_Wv': _L2_xattn_in['Wv'], 'L2_xattn_Wo': _L2_xattn_in['Wo'], 'L3_xattn_Wq': _L3_xattn_in['Wq'], 'L3_xattn_bq': _L3_xattn_in['bq'], 'L3_xattn_Wk': _L3_xattn_in['Wk'], 'L3_xattn_bk': _L3_xattn_in['bk'], 'L3_xattn_Wv': _L3_xattn_in['Wv'], 'L3_xattn_bv': _L3_xattn_in['bv'], 'L3_xattn_Wo': _L3_xattn_in['Wo'], 'L3_xattn_bo': _L3_xattn_in['bo'], 'L3_xattn_ln_g': _L3_xattn_in['ln_g'], 'L3_xattn_ln_b': _L3_xattn_in['ln_b']}

def reference(x, ctx_1024, mask_1xS2_bf0, mask_BxSxS2_ik1, L0_xattn_ln1_g, L0_xattn_ln1_b, L0_xattn_sa_wq, L0_xattn_sa_bq, L0_xattn_sa_wk, L0_xattn_sa_bk, L0_xattn_sa_wv, L0_xattn_sa_bv, L0_xattn_sa_wo, L0_xattn_sa_bo, L0_xattn_ln2_g, L0_xattn_ln2_b, L0_xattn_ca_wq, L0_xattn_ca_bq, L0_xattn_ca_wk, L0_xattn_ca_bk, L0_xattn_ca_wv, L0_xattn_ca_bv, L0_xattn_ca_wo, L0_xattn_ca_bo, L0_xattn_ln3_g, L0_xattn_ln3_b, L0_xattn_fc1_w, L0_xattn_fc1_b, L0_xattn_fc2_w, L0_xattn_fc2_b, L1_xattn_sa_ln_g, L1_xattn_sa_ln_b, L1_xattn_sa_in_w, L1_xattn_sa_in_b, L1_xattn_sa_out_w, L1_xattn_sa_out_b, L1_xattn_ca_q_ln_g, L1_xattn_ca_q_ln_b, L1_xattn_ca_kv_ln_g, L1_xattn_ca_kv_ln_b, L1_xattn_ca_in_w, L1_xattn_ca_in_b, L1_xattn_ca_out_w, L1_xattn_ca_out_b, L1_xattn_moe_ln_g, L1_xattn_moe_ln_b, L1_xattn_router_w, L1_xattn_router_b, L1_xattn_e_fc1_w, L1_xattn_e_fc1_b, L1_xattn_e_fc2_w, L1_xattn_e_fc2_b, L2_xattn_m_norm_w, L2_xattn_in_proj_w, L2_xattn_conv_w, L2_xattn_conv_b, L2_xattn_dt_bias, L2_xattn_A_log, L2_xattn_D_skip, L2_xattn_gnorm_w, L2_xattn_out_proj_w, L2_xattn_ca_ln_w, L2_xattn_ca_ln_b, L2_xattn_Wq, L2_xattn_Wk, L2_xattn_Wv, L2_xattn_Wo, L3_xattn_Wq, L3_xattn_bq, L3_xattn_Wk, L3_xattn_bk, L3_xattn_Wv, L3_xattn_bv, L3_xattn_Wo, L3_xattn_bo, L3_xattn_ln_g, L3_xattn_ln_b):
    import jax
    import jax.numpy as jnp

    def _L0_xattn_ref(x, y, ln1_g, ln1_b, sa_wq, sa_bq, sa_wk, sa_bk, sa_wv, sa_bv, sa_wo, sa_bo, ln2_g, ln2_b, ca_wq, ca_bq, ca_wk, ca_bk, ca_wv, ca_bv, ca_wo, ca_bo, ln3_g, ln3_b, fc1_w, fc1_b, fc2_w, fc2_b):
        import jax, jax.numpy as jnp
        import numpy as np
        B, LX, LY = (2, 256, 256)
        E, H = (128, 16)
        HD = E // H
        FF = 512
        EPS = 1e-05

        def _rope_tables(L, d):
            inv = 1.0 / 10000.0 ** (jnp.arange(0, d, 2, dtype=jnp.float32) / d)
            t = jnp.arange(L, dtype=jnp.float32)
            f = jnp.outer(t, inv)
            return (jnp.cos(f), jnp.sin(f))

        def _apply_rope(x, cos, sin):
            d2 = x.shape[-1] // 2
            x1, x2 = (x[..., :d2], x[..., d2:])
            c = cos[None, :, None, :]
            s = sin[None, :, None, :]
            return jnp.concatenate([x1 * c - x2 * s, x2 * c + x1 * s], axis=-1)

        def _ln(x, g, b):
            m = jnp.mean(x, axis=-1, keepdims=True)
            v = jnp.var(x, axis=-1, keepdims=True)
            return (x - m) / jnp.sqrt(v + EPS) * g + b

        def _attn(q, k, v, causal):
            s = jnp.einsum('blhd,bmhd->bhlm', q, k)
            if causal:
                Lq, Lk = (s.shape[2], s.shape[3])
                mask = jnp.tril(jnp.ones((Lq, Lk), dtype=bool))
                s = jnp.where(mask, s, -jnp.inf)
            p = jax.nn.softmax(s, axis=-1)
            return jnp.einsum('bhlm,bmhd->blhd', p, v)

        def _forward(x, y, ln1_g, ln1_b, sa_wq, sa_bq, sa_wk, sa_bk, sa_wv, sa_bv, sa_wo, sa_bo, ln2_g, ln2_b, ca_wq, ca_bq, ca_wk, ca_bk, ca_wv, ca_bv, ca_wo, ca_bo, ln3_g, ln3_b, fc1_w, fc1_b, fc2_w, fc2_b):
            Bx, Lx, _ = x.shape
            Ly = y.shape[1]
            cos, sin = _rope_tables(max(Lx, Ly), HD)
            scale = HD ** (-0.5)
            h = _ln(x, ln1_g, ln1_b)
            q = (h @ sa_wq + sa_bq).reshape(Bx, Lx, H, HD) * scale
            k = (h @ sa_wk + sa_bk).reshape(Bx, Lx, H, HD)
            v = (h @ sa_wv + sa_bv).reshape(Bx, Lx, H, HD)
            q = _apply_rope(q, cos[:Lx], sin[:Lx])
            k = _apply_rope(k, cos[:Lx], sin[:Lx])
            a = _attn(q, k, v, causal=True).reshape(Bx, Lx, E)
            x = x + (a @ sa_wo + sa_bo)
            h = _ln(x, ln2_g, ln2_b)
            q = (h @ ca_wq + ca_bq).reshape(Bx, Lx, H, HD) * scale
            k = (y @ ca_wk + ca_bk).reshape(Bx, Ly, H, HD)
            v = (y @ ca_wv + ca_bv).reshape(Bx, Ly, H, HD)
            q = _apply_rope(q, cos[:Lx], sin[:Lx])
            k = _apply_rope(k, cos[:Ly], sin[:Ly])
            a = _attn(q, k, v, causal=False).reshape(Bx, Lx, E)
            x = x + (a @ ca_wo + ca_bo)
            h = _ln(x, ln3_g, ln3_b)
            return x + (jax.nn.gelu(h @ fc1_w + fc1_b) @ fc2_w + fc2_b)
        return _forward(x, y, ln1_g, ln1_b, sa_wq, sa_bq, sa_wk, sa_bk, sa_wv, sa_bv, sa_wo, sa_bo, ln2_g, ln2_b, ca_wq, ca_bq, ca_wk, ca_bk, ca_wv, ca_bv, ca_wo, ca_bo, ln3_g, ln3_b, fc1_w, fc1_b, fc2_w, fc2_b)

    def _L1_xattn_ref(latents, tokens, sa_ln_g, sa_ln_b, sa_in_w, sa_in_b, sa_out_w, sa_out_b, ca_q_ln_g, ca_q_ln_b, ca_kv_ln_g, ca_kv_ln_b, ca_in_w, ca_in_b, ca_out_w, ca_out_b, moe_ln_g, moe_ln_b, router_w, router_b, e_fc1_w, e_fc1_b, e_fc2_w, e_fc2_b):
        import jax, jax.numpy as jnp
        import numpy as np
        D, H, E, K, DFF = (128, 16, 8, 2, 512)
        B, L, T = (4, 64, 256)
        EPS = 1e-05

        def _xavier(key, shape):
            fan_in, fan_out = (shape[-1], shape[-2])
            a = jnp.sqrt(6.0 / (fan_in + fan_out))
            return jax.random.uniform(key, shape, jnp.float32, -a, a)

        def _ln(x, g, b):
            m = x.mean(-1, keepdims=True)
            v = ((x - m) ** 2).mean(-1, keepdims=True)
            return (x - m) / jnp.sqrt(v + EPS) * g + b

        def _mha(q_in, kv_in, in_w, in_b, out_w, out_b):
            wq, wk, wv = jnp.split(in_w, 3, axis=0)
            bq, bk, bv = jnp.split(in_b, 3, axis=0)
            dh = D // H

            def heads(x, w, b):
                y = x @ w.T + b
                return y.reshape(x.shape[0], x.shape[1], H, dh).transpose(0, 2, 1, 3)
            q = heads(q_in, wq, bq)
            k = heads(kv_in, wk, bk)
            v = heads(kv_in, wv, bv)
            scores = jnp.einsum('bhqd,bhkd->bhqk', q, k) / jnp.sqrt(jnp.float32(dh))
            attn = jax.nn.softmax(scores, axis=-1)
            out = jnp.einsum('bhqk,bhkd->bhqd', attn, v)
            out = out.transpose(0, 2, 1, 3).reshape(q_in.shape[0], q_in.shape[1], D)
            return out @ out_w.T + out_b

        def _fuse_moe(x, ln_g, ln_b, rw, rb, fc1_w, fc1_b, fc2_w, fc2_b):
            h = _ln(x, ln_g, ln_b)
            logits = h @ rw.T + rb
            vals, idx = jax.lax.top_k(logits, K)
            gates = jax.nn.softmax(vals, axis=-1)
            N = x.shape[0] * x.shape[1]
            hf = h.reshape(N, D)
            h1 = jax.nn.gelu(jnp.einsum('nd,efd->enf', hf, fc1_w) + fc1_b[:, None, :], approximate=False)
            eo = jnp.einsum('enf,edf->end', h1, fc2_w) + fc2_b[:, None, :]
            idx_f = idx.reshape(N, K)
            gates_f = gates.reshape(N, K)
            gathered = eo[idx_f, jnp.arange(N)[:, None], :]
            mixed = (gathered * gates_f[..., None]).sum(axis=1).reshape(x.shape)
            return x + mixed
        q = _ln(latents, sa_ln_g, sa_ln_b)
        x = latents + _mha(q, q, sa_in_w, sa_in_b, sa_out_w, sa_out_b)
        qc = _ln(x, ca_q_ln_g, ca_q_ln_b)
        kv = _ln(tokens, ca_kv_ln_g, ca_kv_ln_b)
        x = x + _mha(qc, kv, ca_in_w, ca_in_b, ca_out_w, ca_out_b)
        return _fuse_moe(x, moe_ln_g, moe_ln_b, router_w, router_b, e_fc1_w, e_fc1_b, e_fc2_w, e_fc2_b)

    def _L2_xattn_ref(x, encoder_out, encoder_padding_mask, m_norm_w, in_proj_w, conv_w, conv_b, dt_bias, A_log, D_skip, gnorm_w, out_proj_w, ca_ln_w, ca_ln_b, Wq, Wk, Wv, Wo):
        import jax, jax.numpy as jnp
        import numpy as np
        D = 128
        D_STATE = 128
        N_HEADS = 8
        D_INNER = 2 * D
        HEADDIM = 64
        H_M = D_INNER // HEADDIM
        D_CONV = 4
        CONV_DIM = D_INNER + 2 * D_STATE
        D_IN_PROJ = 2 * D_INNER + 2 * D_STATE + H_M
        B = 1
        LQ = 128
        LK = 256
        EPS = 1e-05

        def _rms(x, w):
            return x * jax.lax.rsqrt(jnp.mean(x * x, axis=-1, keepdims=True) + EPS) * w

        def _ln(x, w, b):
            mu = jnp.mean(x, axis=-1, keepdims=True)
            v = jnp.mean((x - mu) ** 2, axis=-1, keepdims=True)
            return (x - mu) * jax.lax.rsqrt(v + EPS) * w + b

        def _mamba2_block(x, norm_w, in_proj_w, conv_w, conv_b, dt_bias, A_log, D_skip, gnorm_w, out_proj_w):
            b, L, _ = x.shape
            resid = x
            zxbcdt = _rms(x, norm_w) @ in_proj_w
            z = zxbcdt[..., :D_INNER]
            xBC = zxbcdt[..., D_INNER:D_INNER + CONV_DIM]
            dt = jax.nn.softplus(zxbcdt[..., -H_M:] + dt_bias)
            padded = jnp.pad(xBC, ((0, 0), (D_CONV - 1, 0), (0, 0)))
            conv = conv_b + sum((padded[:, k:k + L, :] * conv_w[:, k] for k in range(D_CONV)))
            xBC = jax.nn.silu(conv)
            xh = xBC[..., :D_INNER].reshape(b, L, H_M, HEADDIM)
            Bm = xBC[..., D_INNER:D_INNER + D_STATE]
            Cm = xBC[..., D_INNER + D_STATE:]
            A = -jnp.exp(A_log)
            decay = jnp.exp(dt * A)
            dbx = dt[..., None] * xh

            def step(h, inp):
                dec, u, bt, ct = inp
                h = h * dec[:, :, None, None] + u[..., None] * bt[:, None, None, :]
                y = jnp.einsum('bhpn,bn->bhp', h, ct)
                return (h, y)
            h0 = jnp.zeros((b, H_M, HEADDIM, D_STATE), x.dtype)
            xs = (decay.transpose(1, 0, 2), dbx.transpose(1, 0, 2, 3), Bm.transpose(1, 0, 2), Cm.transpose(1, 0, 2))
            _, ys = jax.lax.scan(step, h0, xs)
            y = ys.transpose(1, 0, 2, 3) + D_skip[None, None, :, None] * xh
            u = _rms(y.reshape(b, L, D_INNER) * jax.nn.silu(z), gnorm_w)
            return resid + u @ out_proj_w

        def _cross_attention(x, enc, pad_mask, ln_w, ln_b, Wq, Wk, Wv, Wo):
            b, Lq, _ = x.shape
            Lk = enc.shape[1]
            dh = D // N_HEADS
            resid = x
            xn = _ln(x, ln_w, ln_b)
            q = (xn @ Wq).reshape(b, Lq, N_HEADS, dh)
            k = (enc @ Wk).reshape(b, Lk, N_HEADS, dh)
            v = (enc @ Wv).reshape(b, Lk, N_HEADS, dh)
            scores = jnp.einsum('bqhd,bkhd->bhqk', q, k) * np.float32(1.0 / np.sqrt(dh))
            scores = jnp.where(pad_mask[:, None, None, :], jnp.float32(-1000000000.0), scores)
            p = jax.nn.softmax(scores, axis=-1)
            ctx = jnp.einsum('bhqk,bkhd->bqhd', p, v).reshape(b, Lq, D)
            return resid + ctx @ Wo
        h = _mamba2_block(x, m_norm_w, in_proj_w, conv_w, conv_b, dt_bias, A_log, D_skip, gnorm_w, out_proj_w)
        return _cross_attention(h, encoder_out, encoder_padding_mask, ca_ln_w, ca_ln_b, Wq, Wk, Wv, Wo)

    def _L3_xattn_ref(query, key, value, mask, Wq, bq, Wk, bk, Wv, bv, Wo, bo, ln_g, ln_b):
        import jax, jax.numpy as jnp
        import numpy as np
        H = 128
        NH = 16
        HD = H // NH
        EPS = 1e-05

        def _split_heads(x, B, L):
            return x.reshape(B, L, NH, HD).transpose(0, 2, 1, 3)
        B, LQ, _ = query.shape
        LK = key.shape[1]
        Q = _split_heads(query @ Wq.T + bq, B, LQ)
        K = _split_heads(key @ Wk.T + bk, B, LK)
        V = _split_heads(value @ Wv.T + bv, B, LK)
        scores = jnp.einsum('bhqd,bhkd->bhqk', Q, K) / np.sqrt(HD)
        scores = jnp.where(mask[:, None, :, :] == 0, jnp.float32(-1000000000.0), scores)
        attn = jax.nn.softmax(scores, axis=-1)
        ctx = jnp.einsum('bhqk,bhkd->bhqd', attn, V)
        ctx = ctx.transpose(0, 2, 1, 3).reshape(B, LQ, H)
        out = ctx @ Wo.T + bo
        x = out + query
        mu = jnp.mean(x, axis=-1, keepdims=True)
        var = jnp.mean(jnp.square(x - mu), axis=-1, keepdims=True)
        return (x - mu) / jnp.sqrt(var + EPS) * ln_g + ln_b
    x = _L0_xattn_ref(x, ctx_1024, L0_xattn_ln1_g, L0_xattn_ln1_b, L0_xattn_sa_wq, L0_xattn_sa_bq, L0_xattn_sa_wk, L0_xattn_sa_bk, L0_xattn_sa_wv, L0_xattn_sa_bv, L0_xattn_sa_wo, L0_xattn_sa_bo, L0_xattn_ln2_g, L0_xattn_ln2_b, L0_xattn_ca_wq, L0_xattn_ca_bq, L0_xattn_ca_wk, L0_xattn_ca_bk, L0_xattn_ca_wv, L0_xattn_ca_bv, L0_xattn_ca_wo, L0_xattn_ca_bo, L0_xattn_ln3_g, L0_xattn_ln3_b, L0_xattn_fc1_w, L0_xattn_fc1_b, L0_xattn_fc2_w, L0_xattn_fc2_b)
    x = _L1_xattn_ref(x, ctx_1024, L1_xattn_sa_ln_g, L1_xattn_sa_ln_b, L1_xattn_sa_in_w, L1_xattn_sa_in_b, L1_xattn_sa_out_w, L1_xattn_sa_out_b, L1_xattn_ca_q_ln_g, L1_xattn_ca_q_ln_b, L1_xattn_ca_kv_ln_g, L1_xattn_ca_kv_ln_b, L1_xattn_ca_in_w, L1_xattn_ca_in_b, L1_xattn_ca_out_w, L1_xattn_ca_out_b, L1_xattn_moe_ln_g, L1_xattn_moe_ln_b, L1_xattn_router_w, L1_xattn_router_b, L1_xattn_e_fc1_w, L1_xattn_e_fc1_b, L1_xattn_e_fc2_w, L1_xattn_e_fc2_b)
    x = _L2_xattn_ref(x, ctx_1024, mask_1xS2_bf0, L2_xattn_m_norm_w, L2_xattn_in_proj_w, L2_xattn_conv_w, L2_xattn_conv_b, L2_xattn_dt_bias, L2_xattn_A_log, L2_xattn_D_skip, L2_xattn_gnorm_w, L2_xattn_out_proj_w, L2_xattn_ca_ln_w, L2_xattn_ca_ln_b, L2_xattn_Wq, L2_xattn_Wk, L2_xattn_Wv, L2_xattn_Wo)
    x = _L3_xattn_ref(x, ctx_1024, ctx_1024, mask_BxSxS2_ik1, L3_xattn_Wq, L3_xattn_bq, L3_xattn_Wk, L3_xattn_bk, L3_xattn_Wv, L3_xattn_bv, L3_xattn_Wo, L3_xattn_bo, L3_xattn_ln_g, L3_xattn_ln_b)
    return x

_drawn_inputs = setup_inputs


def setup_inputs(seed=0):
    import zlib

    import numpy as np

    out = dict(_drawn_inputs(seed))
    spreads = {'L0_xattn_ln1_g': (1.0, 0.6),
     'L0_xattn_ln1_b': (0.0, 0.403),
     'L0_xattn_sa_bq': (0.0, 0.8),
     'L0_xattn_sa_bk': (0.0, 0.8),
     'L0_xattn_sa_bv': (0.0, 0.1),
     'L0_xattn_sa_bo': (0.0, 0.1),
     'L0_xattn_ln2_g': (1.0, 0.6),
     'L0_xattn_ln2_b': (0.0, 0.8),
     'L0_xattn_ca_bq': (0.0, 0.8),
     'L0_xattn_ca_bk': (0.0, 0.8),
     'L0_xattn_ca_bv': (0.0, 0.1),
     'L0_xattn_ca_bo': (0.0, 0.1),
     'L0_xattn_ln3_g': (1.0, 0.6),
     'L0_xattn_ln3_b': (0.0, 0.445),
     'L0_xattn_fc1_b': (0.0, 0.1),
     'L0_xattn_fc2_b': (0.0, 0.1),
     'L1_xattn_sa_ln_g': (1.0, 0.2),
     'L1_xattn_sa_ln_b': (0.0, 0.1),
     'L1_xattn_sa_in_b': (0.0, 0.1),
     'L1_xattn_sa_out_b': (0.0, 0.1),
     'L1_xattn_ca_q_ln_g': (1.0, 0.2),
     'L1_xattn_ca_q_ln_b': (0.0, 0.44),
     'L1_xattn_ca_kv_ln_g': (1.0, 0.2),
     'L1_xattn_ca_kv_ln_b': (0.0, 0.1),
     'L1_xattn_ca_in_b': (0.0, 0.1),
     'L1_xattn_ca_out_b': (0.0, 0.1),
     'L1_xattn_moe_ln_g': (1.0, 0.2),
     'L1_xattn_moe_ln_b': (0.0, 0.1),
     'L1_xattn_router_b': (0.0, 0.1),
     'L1_xattn_e_fc1_b': (0.0, 0.1),
     'L1_xattn_e_fc2_b': (0.0, 0.1),
     'L2_xattn_m_norm_w': (1.0, 0.2),
     'L2_xattn_conv_b': (0.0, 0.1),
     'L2_xattn_dt_bias': (-4.600165843963623, 0.6),
     'L2_xattn_D_skip': (1.0, 0.2),
     'L2_xattn_gnorm_w': (1.0, 0.2),
     'L2_xattn_ca_ln_w': (1.0, 0.6),
     'L2_xattn_ca_ln_b': (0.0, 0.8),
     'L3_xattn_bq': (0.0, 0.398),
     'L3_xattn_bk': (0.0, 0.8),
     'L3_xattn_bv': (0.0, 0.1),
     'L3_xattn_bo': (0.0, 0.1),
     'L3_xattn_ln_g': (1.0, 0.2),
     'L3_xattn_ln_b': (0.0, 0.1)}
    factors = {'L0_xattn_sa_wq': 8.0,
     'L0_xattn_sa_wk': 8.0,
     'L0_xattn_ca_wq': 8.0,
     'L0_xattn_ca_wk': 8.0,
     'L2_xattn_conv_w': 2.781,
     'L2_xattn_A_log': 8.0,
     'L2_xattn_Wq': 8.0,
     'L2_xattn_Wk': 8.0,
     'L2_xattn_Wv': 2.923,
     'L2_xattn_Wo': 2.898}
    for name, (base, spread) in spreads.items():
        noise = np.random.default_rng([zlib.crc32(name.encode()), seed]).standard_normal(out[name].shape)
        drawn = base * np.exp(spread * noise) if base else spread * noise
        out[name] = jnp.asarray(drawn.astype(out[name].dtype))
    for name, factor in factors.items():
        out[name] = (out[name] * factor).astype(out[name].dtype)
    return out
```

```python
from contextlib import ExitStack
import math

import numpy as np
import concourse.bass as bass
from concourse import mybir

F32 = mybir.dt.float32
BF16 = mybir.dt.bfloat16
I32 = mybir.dt.int32
U8 = mybir.dt.uint8
ALU = mybir.AluOpType
ACT = mybir.ActivationFunctionType
AX = mybir.AxisListType

B, L, LC, D = 64, 128, 77, 128
FF = 512
NE = 8
DI, DS, HM, HP = 256, 128, 4, 64
S, NB = 2, 4
PRESETS = 2
TURNS = B // (S * NB)
FC = FF // 128
DIN = 2 * DI + 2 * DS + HM
EPS = 1e-5
BIG = -(2.0 ** 60)


class Attention:

    def __init__(self, name, heads, keys, wq, wk, wv, wo, bq=None, bk=None, bv=None, bo=None,
                 rope=False, mask=None, norm=None, kv_norm=None):
        self.name, self.heads, self.keys = name, heads, keys
        self.wq, self.wk, self.wv, self.wo = wq, wk, wv, wo
        self.bq, self.bk, self.bv, self.bo = bq, bk, bv, bo
        self.rope, self.mask, self.norm, self.kv_norm = rope, mask, norm, kv_norm
        self.own = keys == L
        self.width = D // heads
        self.halves = heads // 8
        self.quads = heads // 4
        self.scale = self.width ** -0.5


ATT = [
    Attention("L0s", 16, L, "L0_sa_wq", "L0_sa_wk", "L0_sa_wv", "L0_sa_wo", "L0_sa_bq", "L0_sa_bk", "L0_sa_bv",
              "L0_sa_bo", rope=True, mask="causal", norm=0),
    Attention("L0c", 16, LC, "L0_ca_wq", "L0_ca_wk", "L0_ca_wv", "L0_ca_wo", "L0_ca_bq", "L0_ca_bk", "L0_ca_bv",
              "L0_ca_bo", rope=True, norm=1),
    Attention("L1s", 16, L, "L1_sa_wq", "L1_sa_wk", "L1_sa_wv", "L1_sa_wo", "L1_sa_bq", "L1_sa_bk", "L1_sa_bv",
              "L1_sa_bo", norm=3),
    Attention("L1c", 16, LC, "L1_ca_wq", "L1_ca_wk", "L1_ca_wv", "L1_ca_wo", "L1_ca_bq", "L1_ca_bk", "L1_ca_bv",
              "L1_ca_bo", norm=4, kv_norm=5),
    Attention("L2c", 8, LC, "L2_wq", "L2_wk", "L2_wv", "L2_wo", mask="keys", norm=8),
    Attention("L3c", 16, LC, "L3_wq", "L3_wk", "L3_wv", "L3_wo", "L3_bq", "L3_bk", "L3_bv", "L3_bo",
              mask="pairs", norm=9),
]

NORMS = {0: ("L0_ln1_g", "L0_ln1_b"), 1: ("L0_ln2_g", "L0_ln2_b"), 2: ("L0_ln3_g", "L0_ln3_b"),
         3: ("L1_sa_ln_g", "L1_sa_ln_b"), 4: ("L1_ca_q_ln_g", "L1_ca_q_ln_b"),
         5: ("L1_ca_kv_ln_g", "L1_ca_kv_ln_b"), 6: ("L1_moe_ln_g", "L1_moe_ln_b"),
         7: ("L2_m_norm_w", None), 8: ("L2_ca_ln_w", "L2_ca_ln_b"), 9: (None, None), 10: (None, None)}
NORM_KV, NORM_RMS, NORM_NONE, NORM_LAST = 5, 7, 9, 10

WEIGHTS = (["L0_sa_wq", "L0_sa_wqr", "L0_sa_wk", "L0_sa_wkr", "L0_sa_wv", "L0_sa_wo",
            "L0_ca_wq", "L0_ca_wqr", "L0_ca_wk", "L0_ca_wkr", "L0_ca_wv", "L0_ca_wo"]
           + ["L0_fc1", "L0_fc2"]
           + ["L1_sa_wq", "L1_sa_wk", "L1_sa_wv", "L1_sa_wo", "L1_ca_wq", "L1_ca_wk", "L1_ca_wv", "L1_ca_wo",
              "L1_router", "L1_fc1", "L1_fc2"]
           + ["L2_in", "L2_out", "L2_wq", "L2_wk", "L2_wv", "L2_wo", "L3_wq", "L3_wk", "L3_wv", "L3_wo"])
WIDTH = {"L0_fc1": FF, "L0_fc2": FF, "L1_router": NE, "L1_fc1": NE * FF, "L1_fc2": NE * FF, "L2_in": DIN,
         "L2_out": DI}
COLS = ["L0_ln1_g", "L0_ln1_b", "L0_ln2_g", "L0_ln2_b", "L0_ln3_g", "L0_ln3_b", "L0_sa_bq", "L0_sa_bqr",
        "L0_sa_bk", "L0_sa_bkr", "L0_sa_bv", "L0_ca_bq", "L0_ca_bqr", "L0_ca_bk", "L0_ca_bkr", "L0_ca_bv",
        "L1_sa_ln_g", "L1_sa_ln_b", "L1_ca_q_ln_g", "L1_ca_q_ln_b", "L1_ca_kv_ln_g", "L1_ca_kv_ln_b",
        "L1_moe_ln_g", "L1_moe_ln_b", "L1_sa_bq", "L1_sa_bk", "L1_sa_bv", "L1_ca_bq", "L1_ca_bk", "L1_ca_bv",
        "L2_m_norm_w", "L2_ca_ln_w", "L2_ca_ln_b", "L3_bq", "L3_bk", "L3_bv",
        "L0_fc1_b", "L1_fc1_b", "L2_conv_b", "L2_conv_w", "L2_gnorm"]
COL_WIDTH = {"L0_fc1_b": FC, "L1_fc1_b": NE * FC, "L2_conv_b": 4, "L2_conv_w": 16, "L2_gnorm": 2}
ROWS = ["L0_sa_bo", "L0_ca_bo", "L0_fc2_b", "L1_sa_bo", "L1_ca_bo", "L3_bo", "L3_ln_g", "L3_ln_b",
        "L1_router_b", "L2_dt_bias", "L2_A_log", "L2_D"]
ROW_WIDTH = {"L1_router_b": NE, "L2_dt_bias": HM, "L2_A_log": HM, "L2_D": HM}
CONSTS = ["ident", "cos", "sin", "upto", "after", "heads16", "heads8", "earlier", "half"]
CONST_WIDTH = {"heads16": 16, "heads8": 8, "earlier": NE * NE, "half": NB}


def offsets(names, widths, usual=D):
    at, n = {}, 0
    for name in names:
        w = widths.get(name, usual)
        at[name] = (n, w)
        n += w
    return at, n


W_AT, W_N = offsets(WEIGHTS, WIDTH)
C_AT, C_N = offsets(COLS, COL_WIDTH, 1)
R_AT, R_N = offsets(ROWS, ROW_WIDTH)
K_AT, K_N = offsets(CONSTS, CONST_WIDTH)


def norm_steps(n, s):
    return ([("stats", n, s)] if n != NORM_NONE else []) + [("norm", n, s)]


def attention_steps(a):
    t = ATT[a]
    out = []
    for s in range(S):
        out += norm_steps(t.norm, s)
        out.append(("project", a, s, "q"))
        if t.kv_norm is not None:
            out += norm_steps(t.kv_norm, s)
        out += [("project", a, s, "k"), ("values", a, s)]
        if t.bo:
            out.append(("bias", a, s))
    units = [(s, b, h) for s in range(S) for b in range(NB) for h in range(t.halves)]
    for n in range(len(units) + 3):
        if n < len(units):
            s, b, h = units[n]
            if h == 0:
                out.append(("spread", a, s, b))
            out.append(("scores", a, s, b, h))
        if 2 <= n < len(units) + 2:
            s, b, h = units[n - 2]
            out += [("turn", a, s, b, 2 * h + q) for q in range(2)]
        if 3 <= n:
            s, b, h = units[n - 3]
            out += [("mix", a, s, b, 2 * h + q) for q in range(2)]
            if h == t.halves - 1:
                out += [("gather", a, s, b), ("regroup", a, s, b)]
                if b == NB - 1:
                    out += [("turn_out", a, s), ("out", a, s)]
    return out


def schedule():
    out = [("load", s) for s in range(S)]
    out += attention_steps(0) + attention_steps(1)
    for s in range(S):
        out += norm_steps(2, s) + [("bias_mlp", s)]
    for s in range(S):
        out += [("hidden", s, c) for c in range(FC)]
        out += [("mlp", s)]
    out += attention_steps(2) + attention_steps(3)
    for s in range(S):
        out += norm_steps(6, s) + [("route", s), ("gates", s), ("expert_bias", s)]
    units = [(s, e) for s in range(S) for e in range(NE)]
    for n in range(len(units) + 1):
        if n < len(units):
            out += [("up", *units[n], c) for c in range(FC)]
        if n:
            out.append(("down", *units[n - 1]))
    for s in range(S):
        out += norm_steps(7, s) + [("step_size", s), ("step_size2", s)]
        out += [("z", s, h) for h in range(2)]
        out += [("conv", s, c) for c in range(4)]
        out += [("rows", s, h) for h in range(2)]
        out.append(("pairs", s))
        out += [("decay", s, b) for b in range(NB)]
        out += [("scan", s, h) for h in range(2)]
        out += [("gate_stats", s), ("gate_norm", s)]
        out += [("turn_gate", s, c) for c in range(2)]
        out.append(("mamba_out", s))
    out += attention_steps(4) + attention_steps(5)
    for s in range(S):
        out += [("stats", NORM_LAST, s), ("norm", NORM_LAST, s), ("store", s)]
    return out


SCHEDULE = schedule()
ORDINAL = {}
for _step in SCHEDULE:
    ORDINAL[_step] = 1 + sum(k[0] == _step[0] for k in ORDINAL)
assert len(ORDINAL) == len(SCHEDULE)

BANKS = {"scores": ([(0, 1), (2, 3)], "dve"), "turn": ([(4,), (5,)], "act"), "mix": ([(6,)], None),
         "regroup": ([(7,)], "dve"), "norm": ([(7,), (4,), (5,)], "act"), "values": ([(7,), (4,), (5,)], "dve"),
         "turn_out": ([(7,)], "act"), "out": ([(4,), (5,)], "dve"),
         "hidden": ([(0,), (1,), (2,), (3,)], "act"), "mlp": ([(7,)], "dve"),
         "route": ([(7,)], "dve"), "gates": ([(4,)], "act"), "expert_bias": ([(5,)], "dve"),
         "up": ([(0,), (1,), (2,), (3,)], "act"), "down": ([(7,), (5,)], "dve"),
         "step_size": ([(7,)], "dve"), "z": ([(4,), (5,)], "act"), "conv": ([(0,), (1,), (2,), (3,)], "dve"),
         "rows": ([(4,), (5,)], "act"), "pairs": ([(7,)], "dve"), "decay": ([(0,), (1,)], "act"),
         "scan": ([(2,), (3,)], "dve"), "turn_gate": ([(4,), (5,)], "act"), "mamba_out": ([(7,)], "dve")}


def build(nc, x, ctx_rows, ctx_cols, mask_pairs, mask_keys, weights, cols, rows, expert_b2, consts, consts16, out):
    stack = ExitStack()
    with stack:
        def sb(name, shape, dt=F32):
            return stack.enter_context(nc.sbuf_tensor(name, shape, dt))

        sems = {}

        class Signal:

            def __init__(self, name, kind, first=None):
                self.sem = stack.enter_context(nc.semaphore(name))
                self.kind = kind
                sems[name] = self.sem

            def __call__(self, *step):
                return self.sem, ORDINAL[(self.kind, *step)]

        w_sb = sb("w_sb", [128, W_N])
        c_sb = sb("c_sb", [128, C_N])
        r_sb = sb("r_sb", [128, R_N])
        k_sb = sb("k_sb", [128, K_N])
        k16 = sb("k16", [128, 2 * 128], BF16)
        b2_sb = sb("b2_sb", [NE, D])
        mk8 = sb("mk8", [128, LC], U8)
        mk16 = sb("mk16", [128, LC], BF16)
        a_neg = sb("a_neg", [128, HM])

        def W(name, a=0, b=None):
            o, n = W_AT[name]
            return w_sb[:, o + a:o + (n if b is None else b)]

        def C(name, j=0):
            o = C_AT[name][0]
            return c_sb[:, o + j:o + j + 1]

        def R(name):
            o, n = R_AT[name]
            return r_sb[:, o:o + n]

        def K(name):
            o, n = K_AT[name]
            return k_sb[:, o:o + n]

        ident = K("ident")
        ident16 = k16[:, 0:128]
        causal16 = k16[:, 128:256]

        xs = [sb(f"x{s}", [128, NB, D]) for s in range(S)]
        xh = [sb(f"xh{s}", [128, NB, D]) for s in range(S)]
        hT = [sb(f"hT{s}", [128, NB * L]) for s in range(S)]
        qT = [sb(f"qT{s}", [128, NB * L]) for s in range(S)]
        kT = [sb(f"kT{s}", [128, NB * L]) for s in range(S)]
        cx = [sb(f"cx{s}", [LC, NB, D]) for s in range(S)]
        cT = [sb(f"cT{s}", [128, NB * LC]) for s in range(S)]
        v16 = [sb(f"v16_{s}", [128, NB * 16, 32]) for s in range(S)]
        v8 = [sb(f"v8_{s}", [128, NB * 8, 32]) for s in range(S)]
        mp32 = [sb(f"mp32_{s}", [128, NB, LC], I32) for s in range(S)]
        mp16 = [sb(f"mp16_{s}", [128, NB, LC], BF16) for s in range(S)]
        st = [sb(f"st{s}", [128, NB, 6]) for s in range(S)]
        mv = [sb(f"mv{s}", [128, NB, 2]) for s in range(S)]
        var = [sb(f"var{s}", [128, NB]) for s in range(S)]
        rstd = [sb(f"rstd{s}", [128, NB]) for s in range(S)]
        tmp = sb("tmp", [128, NB * L])
        NP, NT = 3, 6
        kx = sb("kx", [128, 2, 16 * L])
        pr = sb("pr", [128, NP, 8 * L])
        pt = sb("pt", [128, NT, 4 * L])
        og = sb("og", [128, 2, 4 * L])
        mx = sb("mx", [128, 2, 8])
        rc = sb("rc", [128, 16])
        h1 = sb("h1", [128, 2, FC * NB * L])
        lg = sb("lg", [128, NB, NE])
        top = sb("top", [128, NB])
        ex = sb("ex", [128, NB, NE])
        beats = sb("beats", [128, NB, NE, NE])
        ties = sb("ties", [128, NB, NE, NE])
        rank = sb("rank", [128, NB, NE])
        gates = [sb(f"gates{s}", [128, NB, NE]) for s in range(S)]
        gT = [sb(f"gT{s}", [NE, NB * L]) for s in range(S)]
        dt_u = sb("dt_u", [128, NB * HM])
        dt_e = sb("dt_e", [128, NB * HM])
        dt_z = sb("dt_z", [128, NB * HM])
        dt_z2 = sb("dt_z2", [128, NB * HM])
        dt_p = sb("dt_p", [128, NB * HM])
        dtv = sb("dtv", [128, NB, HM])
        dta = sb("dta", [128, NB, HM])
        gm = sb("gm", [128, NB, L])
        m1a = sb("m1a", [128, 2, HM * L])
        lw = sb("lw", [128, NB, HM * L])
        ch = h1[:, 0, :].rearrange("p (c t) -> p c t", c=4)
        zg = h1[:, 1, 0:NB * DI].rearrange("p (b i) -> p b i", b=NB)
        xr = h1[:, 1, NB * DI:2 * NB * DI].rearrange("p (b i) -> p b i", b=NB)
        dbx = kx[:, 0, 0:NB * DI].rearrange("p (b i) -> p b i", b=NB)
        dx = kx[:, 0, NB * DI:2 * NB * DI].rearrange("p (b i) -> p b i", b=NB)
        yg = kx[:, 1, 0:NB * DI].rearrange("p (b i) -> p b i", b=NB)
        uT = kx[:, 1, NB * DI:2 * NB * DI].rearrange("p (c t) -> p c t", c=2)

        ps = stack.enter_context(nc.psum_tensor("ps", [128, 8, 512], F32))

        loads = [stack.enter_context(nc.semaphore(f"loads{s}")) for s in range(S)]
        sems.update({f"loads{s}": loads[s] for s in range(S)})
        preset_link = stack.enter_context(nc.semaphore("preset_link"))
        preset = stack.enter_context(nc.semaphore("preset"))
        fetched = stack.enter_context(nc.semaphore("fetched"))
        stored = stack.enter_context(nc.semaphore("stored"))
        arrived = stack.enter_context(nc.semaphore("arrived"))
        cleared = stack.enter_context(nc.semaphore("cleared"))
        go = stack.enter_context(nc.semaphore("go"))
        dve_link = stack.enter_context(nc.semaphore("dve_link"))
        pool_link = stack.enter_context(nc.semaphore("pool_link"))
        sems.update(dve_link=dve_link, pool_link=pool_link)
        mask_ready = Signal("mask_ready", "load")
        variance = Signal("variance", "stats")
        rstd_ready = Signal("rstd_ready", "stats")
        normed = Signal("normed", "norm")
        norm_turned = Signal("norm_turned", "norm")
        hT_ready = Signal("hT_ready", "norm")
        out_rows = Signal("out_rows", "store")
        projected = Signal("projected", "project")
        proj_ready = Signal("proj_ready", "project")
        values_made = Signal("values_made", "values")
        values_ready = Signal("values_ready", "values")
        bias_added = Signal("bias_added", "bias")
        keys_spread = Signal("keys_spread", "spread")
        scores_made = Signal("scores_made", "scores")
        scores_shifted = Signal("scores_shifted", "scores")
        probs_ready = Signal("probs_ready", "scores")
        probs_turned = Signal("probs_turned", "turn")
        probsT_ready = Signal("probsT_ready", "turn")
        mixed = Signal("mixed", "mix")
        gathered = Signal("gathered", "gather")
        regrouped = Signal("regrouped", "regroup")
        heads_ready = Signal("heads_ready", "regroup")
        out_turned = Signal("out_turned", "turn_out")
        outT_ready = Signal("outT_ready", "turn_out")
        out_made = Signal("out_made", "out")
        x_updated = Signal("x_updated", "out")
        mlp_biased = Signal("mlp_biased", "bias_mlp")
        hidden_made = Signal("hidden_made", "hidden")
        hidden_ready = Signal("hidden_ready", "hidden")
        mlp_made = Signal("mlp_made", "mlp")
        mlp_added = Signal("mlp_added", "mlp")
        logits_made = Signal("logits_made", "route")
        logits_ready = Signal("logits_ready", "route")
        route_exp = Signal("route_exp", "route")
        gates_ready = Signal("gates_ready", "gates")
        gates_turned = Signal("gates_turned", "gates")
        gT_ready = Signal("gT_ready", "gates")
        expert_bias_made = Signal("expert_bias_made", "expert_bias")
        expert_bias_added = Signal("expert_bias_added", "expert_bias")
        up_made = Signal("up_made", "up")
        up_ready = Signal("up_ready", "up")
        down_made = Signal("down_made", "down")
        down_added = Signal("down_added", "down")
        dt_made = Signal("dt_made", "step_size")
        dt_abs = Signal("dt_abs", "step_size")
        dt_exp = Signal("dt_exp", "step_size")
        dt_ready = Signal("dt_ready", "step_size2")
        z_made = Signal("z_made", "z")
        z_ready = Signal("z_ready", "z")
        conv_in = Signal("conv_in", "conv")
        conv_done = Signal("conv_done", "conv")
        conv_ready = Signal("conv_ready", "conv")
        rows_made = Signal("rows_made", "rows")
        rows_ready = Signal("rows_ready", "rows")
        rows_scaled = Signal("rows_scaled", "rows")
        pairs_made = Signal("pairs_made", "pairs")
        pairs_ready = Signal("pairs_ready", "pairs")
        decay_in = Signal("decay_in", "decay")
        decay_sums = Signal("decay_sums", "decay")
        decay_exp = Signal("decay_exp", "decay")
        decay_ready = Signal("decay_ready", "decay")
        scan_made = Signal("scan_made", "scan")
        scan_added = Signal("scan_added", "scan")
        scan_gated = Signal("scan_gated", "scan")
        gate_var = Signal("gate_var", "gate_stats")
        gate_rstd = Signal("gate_rstd", "gate_stats")
        gate_normed = Signal("gate_normed", "gate_norm")
        gate_turned = Signal("gate_turned", "turn_gate")
        uT_ready = Signal("uT_ready", "turn_gate")
        mamba_made = Signal("mamba_made", "mamba_out")
        mamba_added = Signal("mamba_added", "mamba_out")

        RELEASED = {"scores": scores_shifted, "turn": probsT_ready, "mix": gathered, "regroup": heads_ready,
                    "norm": hT_ready, "project": proj_ready, "values": values_ready, "turn_out": outT_ready,
                    "out": x_updated, "hidden": hidden_ready, "mlp": mlp_added, "route": logits_ready,
                    "gates": gT_ready, "expert_bias": expert_bias_added, "up": up_ready, "down": down_added,
                    "step_size": dt_abs, "z": z_ready, "conv": conv_done, "rows": rows_ready,
                    "pairs": pairs_ready, "decay": decay_exp, "scan": scan_added, "turn_gate": uT_ready,
                    "mamba_out": mamba_added}

        tile_of, before = {}, {}
        turn_of, last = {}, {}
        for step in SCHEDULE:
            kind = step[0]
            if kind == "project":
                rotate = [(4, 5), (7, 5)] if ATT[step[1]].rope else [(7,), (4,), (5,)]
                key = ("project", len(rotate))
            elif kind in BANKS and not (kind == "norm" and step[1] == NORM_LAST):
                rotate, key = BANKS[kind][0], kind
            else:
                continue
            if kind == "mix" and step[4] > 0:
                tile_of[step] = tile_of[(*step[:4], 0)]
                before[step] = []
                last[tile_of[step][0]] = step
                continue
            n = turn_of.get(key, 0)
            turn_of[key] = n + 1
            tile_of[step] = rotate[n % len(rotate)]
            before[step] = [last[b] for b in tile_of[step] if b in last]
            for b in tile_of[step]:
                last[b] = step

        def wait_bank(pe, step):
            for old in before[step]:
                if old[0] == "mix":
                    pe.wait_ge(*gathered(*old[1:4]))
                else:
                    pe.wait_ge(*RELEASED[old[0]](*old[1:]))

        def bank(step, n=0):
            return ps[:, tile_of[step][n], :]

        def kx_slot(a, s, b):
            return (ORDINAL[("spread", a, s, b)] - 1) % 2

        def pr_slot(step):
            return (ORDINAL[step] - 1) % NP

        def pt_slot(step):
            return (ORDINAL[step] - 1) % NT

        def before_in_ring(kind, step, depth):
            n = ORDINAL[step] - depth
            return KINDS[kind][n - 1] if n > 0 else None

        KINDS = {}
        for step in SCHEDULE:
            KINDS.setdefault(step[0], []).append(step)

        def of_attention(a):
            return ATT[a], ATT[a].keys, (v16 if ATT[a].heads == 16 else v8)

        def source(n, s):
            return (cx[s], LC) if n == NORM_KV else (xs[s], L)

        def loaded(s):
            return loads[s], 4 * 16

        def turn_end(eng, it):
            eng.drain().then_inc(arrived, 1)
            eng.wait_ge(go, it + 1)

        class Link:

            def __init__(self, eng, sem):
                self.eng, self.sem, self.n = eng, sem, 0

            def __call__(self, ins):
                self.n += 1
                ins.then_inc(self.sem, 1)
                self.eng.wait_ge(self.sem, self.n)

        def tell(eng, ins, signal, *step):
            ins.then_inc(signal.sem, 1)
            eng.wait_ge(*signal(*step))

        block = stack.enter_context(nc.Block())

        @block.sync
        def _(sp):
            sp.dma_start(k_sb[:], consts).then_inc(fetched, 16)
            sp.dma_start(k16[:], consts16).then_inc(fetched, 16)
            sp.dma_start(c_sb[:], cols).then_inc(fetched, 16)
            sp.dma_start(r_sb[:], rows.broadcast_to([128, R_N])).then_inc(fetched, 16)
            sp.dma_start(mk8[:], mask_keys.broadcast_to([128, LC])).then_inc(fetched, 16)
            sp.dma_start(b2_sb[:], expert_b2).then_inc(fetched, 16)
            sp.dma_start(w_sb[:], weights).then_inc(fetched, 16)
            with sp.Fori(0, TURNS) as it:
                for s in range(S):
                    first = it * (S * NB) + s * NB
                    sp.dma_start(xs[s][:], x[bass.ds(first, NB)].rearrange("b q d -> q b d")).then_inc(loads[s], 16)
                    sp.dma_start(cx[s][:], ctx_rows[bass.ds(first, NB)].rearrange("b q d -> q b d")).then_inc(loads[s], 16)
                    sp.dma_start(cT[s][:], ctx_cols[:, bass.ds(first * LC, NB * LC)]).then_inc(loads[s], 16)
                    sp.dma_start(mp32[s][:], mask_pairs[bass.ds(first, NB)].rearrange("b q k -> q b k")).then_inc(loads[s], 16)
                for s in range(S):
                    sp.wait_ge(*out_rows(s))
                    sp.dma_start(out[bass.ds(it * (S * NB) + s * NB, NB)].rearrange("b q d -> q b d"),
                                 xh[s][:]).then_inc(stored, 16)
                sp.wait_ge(stored, it * (16 * S) + 16 * S)
                sp.sem_inc(cleared, 1)
                sp.wait_ge(arrived, it * 4 + 4)
                sp.sem_inc(cleared, 1)
                for sem in sems.values():
                    sp.sem_clear(sem)
                sp.sem_inc(go, 1)

        @block.tensor
        def _(pe):
            pe.wait_ge(fetched, 16 * 7)
            pe.wait_ge(preset, PRESETS)
            mm = nc.tensor.matmul
            tr = nc.tensor.transpose
            with pe.Fori(0, TURNS) as it:
                for step in SCHEDULE:
                    kind, args = step[0], step[1:]
                    if step not in tile_of:
                        continue
                    wait_bank(pe, step)
                    p = bank(step)
                    if kind == "norm":
                        n, s = args
                        _, m = source(n, s)
                        if n == NORM_NONE:
                            pe.wait_ge(*x_updated(4, s))
                        else:
                            pe.wait_ge(*normed(n, s))
                        rows_ = xs[s] if n == NORM_NONE else xh[s]
                        for b in range(NB):
                            i = tr(p[:, b * m:(b + 1) * m], rows_[0:m, b, :], ident[0:m, 0:m])
                        i.then_inc(norm_turned.sem, 1)
                    elif kind == "project":
                        a, s, what = args
                        t, keys, _ = of_attention(a)
                        src, n = hT[s], NB * L
                        if what == "k" and not t.own:
                            n = NB * LC
                            if t.kv_norm is None:
                                src = cT[s]
                                pe.wait_ge(*loaded(s))
                        if what == "q" or t.kv_norm is not None:
                            pe.wait_ge(*hT_ready(t.kv_norm if what == "k" else t.norm, s))
                        w = t.wq if what == "q" else t.wk
                        i = mm(p[:, 0:n], W(w), src[:, 0:n], start=True, stop=True)
                        if t.rope:
                            i = mm(bank(step, 1)[:, 0:n], W(w + "r"), src[:, 0:n], start=True, stop=True)
                        i.then_inc(projected.sem, 1)
                    elif kind == "values":
                        a, s = args
                        t, keys, _ = of_attention(a)
                        src = cT[s] if not t.own and t.kv_norm is None else hT[s]
                        for b in range(NB):
                            i = mm(p[0:keys, b * D:(b + 1) * D], src[:, b * keys:(b + 1) * keys], W(t.wv),
                                   start=True, stop=True)
                        i.then_inc(values_made.sem, 1)
                    elif kind == "scores":
                        a, s, b, h = args
                        t, keys, _ = of_attention(a)
                        pe.wait_ge(*keys_spread(a, s, b))
                        pe.wait_ge(*proj_ready(a, s, "q"))
                        mask = {"causal": causal16, "keys": mk16[:], "pairs": mp16[s][:, b, :], None: None}[t.mask]
                        if t.mask == "pairs":
                            pe.wait_ge(*mask_ready(s))
                        k = kx[:, kx_slot(a, s, b), 0:t.heads * keys]
                        for j in range(2):
                            o = bank(step, j)[:, 0:4 * keys]
                            i = mm(o, qT[s][:, b * L:(b + 1) * L], k[:, (8 * h + 4 * j) * keys:(8 * h + 4 * j + 4) * keys],
                                   start=True, stop=mask is None)
                            if mask is not None:
                                i = mm(o.rearrange("p (h k) -> p h k", h=4), ident16,
                                       mask.unsqueeze(1).broadcast_to([128, 4, keys]), start=False, stop=True)
                        i.then_inc(scores_made.sem, 1)
                    elif kind == "turn":
                        a, s, b, q = args
                        t, keys, _ = of_attention(a)
                        unit = ("scores", a, s, b, q // 2)
                        pe.wait_ge(*probs_ready(*unit[1:]))
                        for j in range(4):
                            c = (4 * (q % 2) + j) * keys
                            i = tr(p[0:keys, j * L:(j + 1) * L], pr[:, pr_slot(unit), c:c + keys], ident)
                        i.then_inc(probs_turned.sem, 1)
                    elif kind == "mix":
                        a, s, b, q = args
                        t, keys, v = of_attention(a)
                        pe.wait_ge(*values_ready(a, s))
                        pe.wait_ge(*probsT_ready(a, s, b, q))
                        for j in range(4):
                            i = mm(ps[32 * j:32 * j + 32, tile_of[step][0], q * L:(q + 1) * L],
                                   v[s][0:keys, b * t.heads + 4 * q + j, :],
                                   pt[0:keys, pt_slot(("turn", a, s, b, q)), j * L:(j + 1) * L], start=True, stop=True)
                        i.then_inc(mixed.sem, 1)
                    elif kind == "regroup":
                        a, s, b = args
                        t, keys, _ = of_attention(a)
                        pe.wait_ge(*gathered(a, s, b))
                        for q in range(t.quads):
                            i = tr(p[:, q * L:(q + 1) * L], og[:, ORDINAL[step] % 2, q * L:(q + 1) * L], ident)
                        i.then_inc(regrouped.sem, 1)
                    elif kind == "turn_out":
                        a, s = args
                        pe.wait_ge(*heads_ready(a, s, NB - 1))
                        for b in range(NB):
                            i = tr(p[:, b * L:(b + 1) * L], xh[s][:, b, :], ident)
                        i.then_inc(out_turned.sem, 1)
                    elif kind == "out":
                        a, s = args
                        pe.wait_ge(*outT_ready(a, s))
                        for b in range(NB):
                            i = mm(p[:, b * D:(b + 1) * D], hT[s][:, b * L:(b + 1) * L], W(ATT[a].wo), start=True, stop=True)
                        i.then_inc(out_made.sem, 1)
                    elif kind == "hidden":
                        s, c = args
                        pe.wait_ge(*hT_ready(2, s))
                        mm(p, W("L0_fc1", c * 128, (c + 1) * 128), hT[s][:], start=True, stop=True)\
                            .then_inc(hidden_made.sem, 1)
                    elif kind == "mlp":
                        (s,) = args
                        pe.wait_ge(*hidden_ready(s, FC - 1))
                        for b in range(NB):
                            for c in range(FC):
                                i = mm(p[:, b * D:(b + 1) * D], h1[:, s, c * NB * L + b * L:c * NB * L + (b + 1) * L],
                                       W("L0_fc2", c * D, (c + 1) * D), start=c == 0, stop=c == FC - 1)
                        i.then_inc(mlp_made.sem, 1)
                    elif kind == "route":
                        (s,) = args
                        pe.wait_ge(*hT_ready(6, s))
                        for b in range(NB):
                            i = mm(p[:, b * NE:(b + 1) * NE], hT[s][:, b * L:(b + 1) * L], W("L1_router"), start=True, stop=True)
                        i.then_inc(logits_made.sem, 1)
                    elif kind == "gates":
                        (s,) = args
                        pe.wait_ge(*gates_ready(s))
                        for b in range(NB):
                            i = tr(p[0:NE, b * L:(b + 1) * L], gates[s][:, b, :], ident)
                        i.then_inc(gates_turned.sem, 1)
                    elif kind == "expert_bias":
                        (s,) = args
                        pe.wait_ge(*gT_ready(s))
                        for b in range(NB):
                            i = mm(p[:, b * D:(b + 1) * D], gT[s][:, b * L:(b + 1) * L], b2_sb[:], start=True, stop=True)
                        i.then_inc(expert_bias_made.sem, 1)
                    elif kind == "up":
                        s, e, c = args
                        mm(p, W("L1_fc1", e * FF + c * 128, e * FF + (c + 1) * 128), hT[s][:], start=True, stop=True)\
                            .then_inc(up_made.sem, 1)
                    elif kind == "down":
                        s, e = args
                        pe.wait_ge(*up_ready(s, e, FC - 1))
                        for b in range(NB):
                            for c in range(FC):
                                i = mm(p[:, b * D:(b + 1) * D], h1[:, e % 2, c * NB * L + b * L:c * NB * L + (b + 1) * L],
                                       W("L1_fc2", e * FF + c * D, e * FF + (c + 1) * D), start=c == 0, stop=c == FC - 1)
                        i.then_inc(down_made.sem, 1)
                    elif kind == "step_size":
                        (s,) = args
                        pe.wait_ge(*hT_ready(7, s))
                        for b in range(NB):
                            i = mm(p[:, b * HM:(b + 1) * HM], hT[s][:, b * L:(b + 1) * L], W("L2_in", DIN - HM, DIN),
                                   start=True, stop=True)
                        i.then_inc(dt_made.sem, 1)
                    elif kind == "z":
                        s, h = args
                        for j in range(2):
                            b = 2 * h + j
                            i = mm(p[:, j * DI:(j + 1) * DI], hT[s][:, b * L:(b + 1) * L], W("L2_in", 0, DI), start=True, stop=True)
                        i.then_inc(z_made.sem, 1)
                    elif kind == "conv":
                        s, c = args
                        mm(p, W("L2_in", DI + c * 128, DI + (c + 1) * 128), hT[s][:], start=True, stop=True)\
                            .then_inc(conv_in.sem, 1)
                    elif kind == "rows":
                        s, h = args
                        pe.wait_ge(*conv_ready(s, 1))
                        for j in range(2):
                            for c in range(2):
                                i = tr(p[:, j * DI + c * 128:j * DI + (c + 1) * 128],
                                       ch[:, c, (2 * h + j) * L:(2 * h + j + 1) * L], ident)
                        i.then_inc(rows_made.sem, 1)
                    elif kind == "pairs":
                        (s,) = args
                        pe.wait_ge(*conv_ready(s, 3))
                        for b in range(NB):
                            i = mm(p[:, b * L:(b + 1) * L], ch[:, 2, b * L:(b + 1) * L], ch[:, 3, b * L:(b + 1) * L],
                                   start=True, stop=True)
                        i.then_inc(pairs_made.sem, 1)
                    elif kind == "decay":
                        s, b = args
                        pe.wait_ge(*decay_in(s, b))
                        mm(p, K("after"), m1a[:, b % 2, :], start=True, stop=True).then_inc(decay_sums.sem, 1)
                    elif kind == "scan":
                        s, h = args
                        pe.wait_ge(*decay_ready(s, 2 * h + 1))
                        pe.wait_ge(*rows_scaled(s, h))
                        for j in range(2):
                            b = 2 * h + j
                            for g in range(HM):
                                i = mm(p[:, j * DI + g * HP:j * DI + (g + 1) * HP], lw[:, b, g * L:(g + 1) * L],
                                       dbx[:, b, g * HP:(g + 1) * HP], start=True, stop=True)
                        i.then_inc(scan_made.sem, 1)
                    elif kind == "turn_gate":
                        s, c = args
                        pe.wait_ge(*gate_normed(s))
                        for b in range(NB):
                            i = tr(p[:, b * L:(b + 1) * L], yg[:, b, c * 128:(c + 1) * 128], ident)
                        i.then_inc(gate_turned.sem, 1)
                    elif kind == "mamba_out":
                        (s,) = args
                        pe.wait_ge(*uT_ready(s, 1))
                        for b in range(NB):
                            for c in range(2):
                                i = mm(p[:, b * D:(b + 1) * D], uT[:, c, b * L:(b + 1) * L], W("L2_out", c * D, (c + 1) * D),
                                       start=c == 0, stop=c == 1)
                        i.then_inc(mamba_made.sem, 1)
                    else:
                        raise AssertionError(kind)
                turn_end(pe, it)

        @block.scalar
        def _(act):
            act.wait_ge(fetched, 16 * 7)
            nc.scalar.activation(a_neg[:], R("L2_A_log"), ACT.Exp).then_inc(preset, 1)
            act.wait_ge(preset, PRESETS)
            go_act = nc.scalar.activation
            with act.Fori(0, TURNS) as it:
                for step in SCHEDULE:
                    kind, args = step[0], step[1:]
                    p = bank(step) if step in tile_of else None
                    if kind == "norm":
                        n, s = args
                        if n == NORM_LAST:
                            continue
                        _, m = source(n, s)
                        gain, bias = NORMS[n]
                        act.wait_ge(*norm_turned(n, s))
                        o, i = hT[s][:, 0:NB * m], p[:, 0:NB * m]
                        if gain is None:
                            go_act(o, i, ACT.Copy).then_inc(hT_ready.sem, 1)
                        elif bias is None:
                            go_act(o, i, ACT.Copy, scale=C(gain)).then_inc(hT_ready.sem, 1)
                        else:
                            go_act(o, i, ACT.Identity, scale=C(gain), bias=C(bias)).then_inc(hT_ready.sem, 1)
                    elif kind == "project":
                        a, s, what = args
                        t, keys, _ = of_attention(a)
                        if t.rope:
                            continue
                        n = NB * (L if what == "q" else keys)
                        dst = (qT if what == "q" else kT)[s]
                        act.wait_ge(*projected(*args))
                        bias = t.bq if what == "q" else t.bk
                        if what == "k" and a:
                            act.wait_ge(*keys_spread(a - 1, s, NB - 1))
                        if bias:
                            go_act(dst[:, 0:n], p[:, 0:n], ACT.Identity, bias=C(bias)).then_inc(proj_ready.sem, 1)
                        else:
                            go_act(dst[:, 0:n], p[:, 0:n], ACT.Copy).then_inc(proj_ready.sem, 1)
                    elif kind == "scores":
                        a, s, b, h = args
                        t, keys, _ = of_attention(a)
                        act.wait_ge(*scores_shifted(*args))
                        v = pr[:, pr_slot(step), 0:8 * keys]
                        go_act(v, v, ACT.Exp, scale=t.scale).then_inc(probs_ready.sem, 1)
                    elif kind == "turn":
                        a, s, b, q = args
                        t, keys, _ = of_attention(a)
                        old = before_in_ring("turn", step, NT)
                        if old:
                            act.wait_ge(*mixed(*old[1:]))
                        act.wait_ge(*probs_turned(*args))
                        go_act(pt[0:keys, pt_slot(step), :], p[0:keys, :], ACT.Copy).then_inc(probsT_ready.sem, 1)
                    elif kind == "gather":
                        a, s, b = args
                        t, keys, _ = of_attention(a)
                        act.wait_ge(*mixed(a, s, b, t.quads - 1))
                        old = before_in_ring("gather", step, 2)
                        if old:
                            act.wait_ge(*regrouped(*old[1:]))
                        tile = bank(("mix", a, s, b, 0))
                        go_act(og[:, ORDINAL[step] % 2, 0:t.quads * L], tile[:, 0:t.quads * L], ACT.Copy)\
                            .then_inc(gathered.sem, 1)
                    elif kind == "turn_out":
                        a, s = args
                        bias = ATT[a].bv
                        act.wait_ge(*out_turned(a, s))
                        act.wait_ge(*values_made(a, s))
                        if bias:
                            go_act(hT[s][:], p, ACT.Identity, bias=C(bias)).then_inc(outT_ready.sem, 1)
                        else:
                            go_act(hT[s][:], p, ACT.Copy).then_inc(outT_ready.sem, 1)
                    elif kind == "hidden":
                        s, c = args
                        act.wait_ge(*hidden_made(s, c))
                        go_act(h1[:, s, c * NB * L:(c + 1) * NB * L], p, ACT.Gelu_apprx_tanh, bias=C("L0_fc1_b", c))\
                            .then_inc(hidden_ready.sem, 1)
                    elif kind == "route":
                        (s,) = args
                        act.wait_ge(*logits_ready(s))
                        go_act(ex[:], lg[:], ACT.Exp).then_inc(route_exp.sem, 1)
                    elif kind == "gates":
                        (s,) = args
                        act.wait_ge(*gates_turned(s))
                        go_act(gT[s][:], p[0:NE, :], ACT.Copy).then_inc(gT_ready.sem, 1)
                    elif kind == "up":
                        s, e, c = args
                        if (s, e) >= (0, 2) and c == 0:
                            act.wait_ge(*down_made(*((s, e - 2) if e >= 2 else (s - 1, e + NE - 2))))
                        act.wait_ge(*up_made(s, e, c))
                        go_act(h1[:, e % 2, c * NB * L:(c + 1) * NB * L], p, ACT.Gelu, bias=C("L1_fc1_b", e * FC + c))\
                            .then_inc(up_ready.sem, 1)
                    elif kind == "step_size":
                        (s,) = args
                        act.wait_ge(*dt_abs(s))
                        go_act(dt_e[:], dt_e[:], ACT.Exp, scale=-1.0).then_inc(dt_exp.sem, 1)
                    elif kind == "z":
                        s, h = args
                        act.wait_ge(*z_made(s, h))
                        if s:
                            act.wait_ge(*scan_gated(s - 1, 1))
                        else:
                            act.wait_ge(*down_made(S - 1, NE - 1))
                        go_act(zg[:, 2 * h:2 * h + 2, :], p, ACT.Silu).then_inc(z_ready.sem, 1)
                    elif kind == "conv":
                        s, c = args
                        act.wait_ge(*conv_done(s, c))
                        go_act(ch[:, c, :], ch[:, c, :], ACT.Silu).then_inc(conv_ready.sem, 1)
                    elif kind == "rows":
                        s, h = args
                        act.wait_ge(*rows_made(s, h))
                        if s:
                            act.wait_ge(*rows_scaled(s - 1, 1))
                        go_act(xr[:, 2 * h:2 * h + 2, :], p, ACT.Copy).then_inc(rows_ready.sem, 1)
                    elif kind == "decay":
                        s, b = args
                        act.wait_ge(*decay_sums(s, b))
                        if s:
                            act.wait_ge(*scan_made(s - 1, 1))
                        go_act(lw[:, b, :], p, ACT.Exp).then_inc(decay_exp.sem, 1)
                    elif kind == "turn_gate":
                        s, c = args
                        act.wait_ge(*gate_turned(s, c))
                        if s:
                            act.wait_ge(*mamba_made(s - 1))
                        go_act(uT[:, c, :], p, ACT.Copy, scale=C("L2_gnorm", c)).then_inc(uT_ready.sem, 1)
                turn_end(act, it)

        @block.vector
        def _(dve):
            link = Link(dve, preset_link)
            for t, hd in [(v, 8) for v in v16] + [(v, 16) for v in v8]:
                link(nc.vector.memset(t[:], 0.0))
                link(nc.vector.memset(t[:, :, hd:hd + 1], 1.0))
            dve.wait_ge(fetched, 16 * 7)
            nc.vector.tensor_scalar(mk16[:], mk8[:], 0.0, BIG, ALU.not_equal, ALU.mult).then_inc(preset, 1)
            dve.wait_ge(preset, PRESETS)
            link = Link(dve, dve_link)
            v_ = nc.vector
            with dve.Fori(0, TURNS) as it:
                for step in SCHEDULE:
                    kind, args = step[0], step[1:]
                    p = bank(step) if step in tile_of else None
                    if kind == "load":
                        (s,) = args
                        dve.wait_ge(*loaded(s))
                        tell(dve, v_.tensor_scalar(mp16[s][:], mp32[s][:], 0.0, BIG, ALU.is_equal, ALU.mult), mask_ready, s)
                    elif kind == "stats":
                        n, s = args
                        src, m = source(n, s)
                        if n in (0, NORM_KV):
                            dve.wait_ge(*loaded(s))
                        for b in range(NB):
                            link(v_.bn_stats(st[s][0:m, b, :], src[0:m, b, :]))
                        for b in range(NB):
                            link(v_.bn_aggr(mv[s][0:m, b, :], st[s][0:m, b, :]))
                        if n == NORM_RMS:
                            link(v_.tensor_tensor(var[s][:], mv[s][:, :, 0], mv[s][:, :, 0], ALU.mult))
                            link(v_.tensor_tensor(var[s][:], var[s][:], mv[s][:, :, 1], ALU.add))
                            tell(dve, v_.tensor_scalar(var[s][:], var[s][:], EPS, None, ALU.add), variance, n, s)
                        else:
                            tell(dve, v_.tensor_scalar(var[s][0:m], mv[s][0:m, :, 1], EPS, None, ALU.add), variance, n, s)
                    elif kind == "norm":
                        n, s = args
                        if n == NORM_NONE:
                            tell(dve, v_.tensor_copy(rc[:, 0:1], mx[:, 0, 0:1]), normed, n, s)
                            continue
                        src, m = source(n, s)
                        dve.wait_ge(*rstd_ready(n, s))
                        if n == NORM_KV:
                            dve.wait_ge(*norm_turned(4, s))
                        for b in range(NB):
                            if n == NORM_RMS:
                                i = v_.tensor_scalar(xh[s][:, b, :], src[:, b, :], rstd[s][:, b:b + 1], None, ALU.mult)
                            else:
                                i = v_.tensor_scalar(xh[s][0:m, b, :], src[0:m, b, :], mv[s][0:m, b, 0:1],
                                                     rstd[s][0:m, b:b + 1], ALU.subtract, ALU.mult)
                            if b < NB - 1:
                                link(i)
                        tell(dve, i, normed, n, s)
                    elif kind == "project":
                        a, s, what = args
                        t, keys, _ = of_attention(a)
                        if not t.rope:
                            continue
                        m = L if what == "q" else keys
                        dst = (qT if what == "q" else kT)[s]
                        if what == "k" and a:
                            dve.wait_ge(*keys_spread(a - 1, s, NB - 1))
                        dve.wait_ge(*projected(*args))
                        bias = t.bq if what == "q" else t.bk

                        def by_batch(ap):
                            return ap[:, 0:NB * m].rearrange("p (b t) -> p b t", b=NB)

                        def table(name):
                            return K(name)[:, 0:m].unsqueeze(1).broadcast_to([128, NB, m])
                        link(v_.scalar_tensor_tensor(by_batch(dst[:]), by_batch(p), C(bias), table("cos"), ALU.add, ALU.mult))
                        link(v_.scalar_tensor_tensor(by_batch(tmp[:]), by_batch(bank(step, 1)), C(bias + "r"), table("sin"),
                                                     ALU.add, ALU.mult))
                        tell(dve, v_.tensor_tensor(dst[:, 0:NB * m], dst[:, 0:NB * m], tmp[:, 0:NB * m], ALU.add),
                             proj_ready, *args)
                    elif kind == "values":
                        a, s = args
                        t, keys, v = of_attention(a)
                        dve.wait_ge(*values_made(a, s))
                        tell(dve, v_.tensor_copy(v[s][0:keys, :, 0:t.width],
                                                 p[0:keys, :].rearrange("p (n d) -> p n d", d=t.width)), values_ready, a, s)
                    elif kind == "scores":
                        a, s, b, h = args
                        t, keys, _ = of_attention(a)
                        dve.wait_ge(*scores_made(*args))
                        m = mx[:, ORDINAL[step] % 2, :]
                        lo = tile_of[step][0]
                        tile = ps[:, lo:lo + 2, 0:4 * keys].rearrange("p c (h k) -> p c h k", h=4)
                        link(v_.tensor_reduce(m, tile, AX.X, ALU.max, negate=True))
                        old = before_in_ring("scores", step, NP)
                        if old:
                            for q in range(2):
                                dve.wait_ge(*probs_turned(*old[1:4], 2 * old[4] + q))
                        dst = pr[:, pr_slot(step), 0:8 * keys].rearrange("p (c h k) -> p c h k", c=2, h=4)
                        tell(dve, v_.tensor_tensor(
                            dst, tile, m.rearrange("p (c h) -> p c h", c=2).unsqueeze(3).broadcast_to([128, 2, 4, keys]),
                            ALU.add), scores_shifted, *args)
                    elif kind == "regroup":
                        a, s, b = args
                        t, keys, _ = of_attention(a)
                        dve.wait_ge(*regrouped(a, s, b))
                        tile = p[:, 0:t.heads * 32].rearrange("p (h w) -> p h w", w=32)
                        link(v_.reciprocal(rc[:, 0:t.heads], tile[:, :, t.width]))
                        tell(dve, v_.tensor_tensor(xh[s][:, b, :].rearrange("p (h w) -> p h w", w=t.width),
                                                   tile[:, :, 0:t.width],
                                                   rc[:, 0:t.heads].unsqueeze(2).broadcast_to([128, t.heads, t.width]),
                                                   ALU.mult), heads_ready, a, s, b)
                    elif kind in ("out", "mlp", "expert_bias", "mamba_out"):
                        s = args[-1]
                        made, added = {"out": (out_made, x_updated), "mlp": (mlp_made, mlp_added),
                                       "expert_bias": (expert_bias_made, expert_bias_added),
                                       "mamba_out": (mamba_made, mamba_added)}[kind]
                        dve.wait_ge(*made(*args))
                        if kind == "out" and ATT[args[0]].bo:
                            dve.wait_ge(*bias_added(*args))
                        if kind == "mlp":
                            dve.wait_ge(*mlp_biased(s))
                        flat = xs[s][:].rearrange("p b d -> p (b d)")
                        tell(dve, v_.tensor_tensor(flat, p, flat, ALU.add), added, *args)
                    elif kind == "route":
                        (s,) = args
                        dve.wait_ge(*logits_made(s))
                        link(v_.tensor_tensor(lg[:], p[:, 0:NB * NE].rearrange("p (b e) -> p b e", b=NB),
                                              R("L1_router_b").unsqueeze(1).broadcast_to([128, NB, NE]), ALU.add))
                        link(v_.tensor_reduce(top[:], lg[:], AX.X, ALU.max))
                        tell(dve, v_.tensor_tensor(lg[:], lg[:], top[:].unsqueeze(2).broadcast_to([128, NB, NE]),
                                                   ALU.subtract), logits_ready, s)
                    elif kind == "gates":
                        (s,) = args
                        rows_ = lg[:].unsqueeze(2).broadcast_to([128, NB, NE, NE])
                        cols_ = lg[:].unsqueeze(3).broadcast_to([128, NB, NE, NE])
                        link(v_.tensor_tensor(beats[:], rows_, cols_, ALU.is_gt))
                        link(v_.tensor_tensor(ties[:], rows_, cols_, ALU.is_equal))
                        link(v_.tensor_tensor(ties[:].rearrange("p b e f -> p b (e f)"), ties[:].rearrange("p b e f -> p b (e f)"),
                                              K("earlier").unsqueeze(1).broadcast_to([128, NB, NE * NE]), ALU.mult))
                        link(v_.tensor_tensor(beats[:], beats[:], ties[:], ALU.add))
                        link(v_.tensor_reduce(rank[:], beats[:], AX.X, ALU.add))
                        dve.wait_ge(*route_exp(s))
                        link(v_.scalar_tensor_tensor(rank[:], rank[:], 1.5, ex[:], ALU.is_lt, ALU.mult))
                        link(v_.tensor_reduce(top[:], rank[:], AX.X, ALU.add))
                        link(v_.reciprocal(top[:], top[:]))
                        tell(dve, v_.tensor_tensor(gates[s][:], rank[:], top[:].unsqueeze(2).broadcast_to([128, NB, NE]),
                                                   ALU.mult), gates_ready, s)
                    elif kind == "down":
                        s, e = args
                        dve.wait_ge(*down_made(s, e))
                        for b in range(NB):
                            i = v_.scalar_tensor_tensor(xs[s][:, b, :], p[:, b * D:(b + 1) * D], gates[s][:, b, e:e + 1],
                                                        xs[s][:, b, :], ALU.mult, ALU.add)
                            if b < NB - 1:
                                link(i)
                        tell(dve, i, down_added, s, e)
                    elif kind == "step_size":
                        (s,) = args
                        dve.wait_ge(*dt_made(s))
                        if s:
                            dve.wait_ge(*decay_in(s - 1, NB - 1))
                            dve.wait_ge(*rows_scaled(s - 1, 1))
                        link(v_.tensor_tensor(dt_u[:].rearrange("p (b h) -> p b h", b=NB),
                                              p[:, 0:NB * HM].rearrange("p (b h) -> p b h", b=NB),
                                              R("L2_dt_bias").unsqueeze(1).broadcast_to([128, NB, HM]), ALU.add))
                        tell(dve, v_.scalar_tensor_tensor(dt_e[:], dt_u[:], -1.0, dt_u[:], ALU.mult, ALU.max), dt_abs, s)
                    elif kind == "step_size2":
                        (s,) = args
                        dve.wait_ge(*dt_exp(s))
                        link(v_.tensor_scalar(dt_z[:], dt_e[:], 2.0, None, ALU.add))
                        link(v_.reciprocal(dt_z[:], dt_z[:]))
                        link(v_.tensor_tensor(dt_z[:], dt_z[:], dt_e[:], ALU.mult))
                        link(v_.tensor_tensor(dt_z2[:], dt_z[:], dt_z[:], ALU.mult))
                        link(v_.tensor_scalar(dt_p[:], dt_z2[:], 1.0 / 13, None, ALU.mult))
                        for c in (11, 9, 7, 5, 3):
                            link(v_.scalar_tensor_tensor(dt_p[:], dt_p[:], 1.0 / c, dt_z2[:], ALU.add, ALU.mult))
                        link(v_.scalar_tensor_tensor(dt_p[:], dt_p[:], 1.0, dt_z[:], ALU.add, ALU.mult))
                        link(v_.tensor_scalar(dt_u[:], dt_u[:], 0.0, None, ALU.max))
                        flat = dtv[:].rearrange("p b h -> p (b h)")
                        link(v_.scalar_tensor_tensor(flat, dt_p[:], 2.0, dt_u[:], ALU.mult, ALU.add))
                        tell(dve, v_.scalar_tensor_tensor(dta[:], dtv[:], -1.0, a_neg[:].unsqueeze(1).broadcast_to([128, NB, HM]),
                                                          ALU.mult, ALU.mult), dt_ready, s)
                    elif kind == "conv":
                        s, c = args
                        if s:
                            dve.wait_ge(*rows_made(s - 1, 1))
                            dve.wait_ge(*pairs_made(s - 1))
                        else:
                            dve.wait_ge(*down_made(S - 1, NE - 1))
                        dve.wait_ge(*conv_in(s, c))
                        taps = [C("L2_conv_w", 4 * c + j) for j in range(4)]
                        src = p.rearrange("p (b t) -> p b t", b=NB)
                        dst = ch[:, c, :].rearrange("p (b t) -> p b t", b=NB)
                        link(v_.tensor_scalar(ch[:, c, :], p, taps[3], C("L2_conv_b", c), ALU.mult, ALU.add))
                        for j in (1, 2, 3):
                            i = v_.scalar_tensor_tensor(dst[:, :, j:L], src[:, :, 0:L - j], taps[3 - j], dst[:, :, j:L],
                                                        ALU.mult, ALU.add)
                            if j < 3:
                                link(i)
                        tell(dve, i, conv_done, s, c)
                    elif kind == "pairs":
                        (s,) = args
                        dve.wait_ge(*pairs_made(s))
                        if s:
                            dve.wait_ge(*decay_ready(s - 1, NB - 1))
                        tell(dve, v_.tensor_tensor(gm[:], p.rearrange("p (b t) -> p b t", b=NB),
                                                   K("upto").unsqueeze(1).broadcast_to([128, NB, L]), ALU.mult),
                             pairs_ready, s)
                    elif kind == "scan":
                        s, h = args
                        dve.wait_ge(*scan_made(s, h))
                        dve.wait_ge(*rows_scaled(s, h))
                        if s:
                            dve.wait_ge(*gate_turned(s - 1, 1))
                        tell(dve, v_.tensor_tensor(yg[:, 2 * h:2 * h + 2, :].rearrange("p b i -> p (b i)"), p,
                                                   dx[:, 2 * h:2 * h + 2, :].rearrange("p b i -> p (b i)"), ALU.add),
                             scan_added, s, h)
                    elif kind == "gate_stats":
                        (s,) = args
                        dve.wait_ge(*scan_gated(s, 1))
                        for b in range(NB):
                            link(v_.bn_stats(st[s][:, b, :], yg[:, b, :]))
                        for b in range(NB):
                            link(v_.bn_aggr(mv[s][:, b, :], st[s][:, b, :]))
                        link(v_.tensor_tensor(var[s][:], mv[s][:, :, 0], mv[s][:, :, 0], ALU.mult))
                        link(v_.tensor_tensor(var[s][:], var[s][:], mv[s][:, :, 1], ALU.add))
                        tell(dve, v_.tensor_scalar(var[s][:], var[s][:], EPS, None, ALU.add), gate_var, s)
                    elif kind == "gate_norm":
                        (s,) = args
                        dve.wait_ge(*gate_rstd(s))
                        for b in range(NB):
                            i = v_.tensor_scalar(yg[:, b, :], yg[:, b, :], rstd[s][:, b:b + 1], None, ALU.mult)
                            if b < NB - 1:
                                link(i)
                        tell(dve, i, gate_normed, s)
                turn_end(dve, it)

        @block.gpsimd
        def _(pool):
            def spread_decay(s, b):
                tell(pool, g_.tensor_tensor(m1a[:, b % 2, :].rearrange("p (h t) -> p h t", h=HM),
                                            K("upto").unsqueeze(1).broadcast_to([128, HM, L]),
                                            dta[:, b, :].unsqueeze(2).broadcast_to([128, HM, L]), ALU.mult),
                     decay_in, s, b)

            pool.wait_ge(fetched, 16 * 7)
            pool.wait_ge(preset, PRESETS)
            link = Link(pool, pool_link)
            g_ = nc.gpsimd
            with pool.Fori(0, TURNS) as it:
                for step in SCHEDULE:
                    kind, args = step[0], step[1:]
                    if kind == "stats":
                        n, s = args
                        _, m = source(n, s)
                        pool.wait_ge(*variance(n, s))
                        tell(pool, g_.tensor_tensor(rstd[s][0:m], var[s][0:m], K("half")[0:m], ALU.pow), rstd_ready, n, s)
                    elif kind == "gate_stats":
                        (s,) = args
                        pool.wait_ge(*gate_var(s))
                        tell(pool, g_.tensor_tensor(rstd[s][:], var[s][:], K("half"), ALU.pow), gate_rstd, s)
                    elif kind in ("bias", "bias_mlp"):
                        s = args[-1]
                        n = ATT[args[0]].norm if kind == "bias" else 2
                        row = ATT[args[0]].bo if kind == "bias" else "L0_fc2_b"
                        if n == NORM_NONE:
                            pool.wait_ge(*norm_turned(n, s))
                        else:
                            pool.wait_ge(*normed(n, s))
                        tell(pool, g_.tensor_tensor(xs[s][:], xs[s][:], R(row).unsqueeze(1).broadcast_to([128, NB, D]),
                                                    ALU.add), bias_added if kind == "bias" else mlp_biased, *args)
                    elif kind == "spread":
                        a, s, b = args
                        t, keys, _ = of_attention(a)
                        pool.wait_ge(*proj_ready(a, s, "k"))
                        old = before_in_ring("spread", step, 2)
                        if old:
                            pool.wait_ge(*scores_made(*old[1:], ATT[old[1]].halves - 1))
                        if a == 4 and s == 0 and b < 2:
                            pool.wait_ge(*mamba_made(S - 1))
                        dst = kx[:, kx_slot(a, s, b), 0:t.heads * keys].rearrange("p (h k) -> p h k", h=t.heads)
                        tell(pool, g_.tensor_tensor(
                            dst, kT[s][:, b * keys:(b + 1) * keys].unsqueeze(1).broadcast_to([128, t.heads, keys]),
                            K("heads16" if t.heads == 16 else "heads8").unsqueeze(2).broadcast_to([128, t.heads, keys]),
                            ALU.mult), keys_spread, a, s, b)
                    elif kind == "rows":
                        s, h = args
                        pool.wait_ge(*rows_ready(s, h))
                        pool.wait_ge(*dt_ready(s))
                        if s:
                            pool.wait_ge(*scan_added(s - 1, 1))
                        for j in range(2):
                            b = 2 * h + j
                            v = xr[:, b, :].rearrange("p (h w) -> p h w", h=HM)
                            link(g_.tensor_tensor(dbx[:, b, :].rearrange("p (h w) -> p h w", h=HM), v,
                                                  dtv[:, b, :].unsqueeze(2).broadcast_to([128, HM, HP]), ALU.mult))
                            i = g_.tensor_tensor(dx[:, b, :].rearrange("p (h w) -> p h w", h=HM), v,
                                                 R("L2_D").unsqueeze(2).broadcast_to([128, HM, HP]), ALU.mult)
                            if j == 0:
                                link(i)
                        tell(pool, i, rows_scaled, s, h)
                    elif kind == "decay":
                        s, b = args
                        if b == 0:
                            pool.wait_ge(*dt_ready(s))
                            spread_decay(s, 0)
                        if b + 1 < NB:
                            spread_decay(s, b + 1)
                        pool.wait_ge(*decay_exp(s, b))
                        pool.wait_ge(*pairs_ready(s))
                        v = lw[:, b, :].rearrange("p (h t) -> p h t", h=HM)
                        tell(pool, g_.tensor_tensor(v, v, gm[:, b, :].unsqueeze(1).broadcast_to([128, HM, L]), ALU.mult),
                             decay_ready, s, b)
                    elif kind == "scan":
                        s, h = args
                        pool.wait_ge(*scan_added(s, h))
                        pool.wait_ge(*z_ready(s, h))
                        v = yg[:, 2 * h:2 * h + 2, :]
                        tell(pool, g_.tensor_tensor(v, v, zg[:, 2 * h:2 * h + 2, :], ALU.mult), scan_gated, s, h)
                    elif kind == "store":
                        (s,) = args
                        pool.wait_ge(*normed(NORM_LAST, s))
                        link(g_.tensor_tensor(xh[s][:], xh[s][:], R("L3_ln_g").unsqueeze(1).broadcast_to([128, NB, D]), ALU.mult))
                        tell(pool, g_.tensor_tensor(xh[s][:], xh[s][:], R("L3_ln_b").unsqueeze(1).broadcast_to([128, NB, D]),
                                                    ALU.add), out_rows, s)
                turn_end(pool, it)


def _swap_halves(a):
    return a.reshape(*a.shape[:-1], 16, 2, 4)[..., ::-1, :].reshape(a.shape)


def _blocks(a, n):
    return a.reshape(n, 128, -1).transpose(1, 0, 2).reshape(128, -1)


def _constants():
    ident = np.eye(128, dtype=np.float32)
    inverse = np.float32(1.0) / np.float32(10000.0) ** (np.arange(0, 8, 2, dtype=np.float32) / np.float32(8))
    angle = np.outer(np.arange(128, dtype=np.float32), inverse.astype(np.float32)).astype(np.float32)
    feature = np.arange(128)
    cos = np.cos(angle).T[feature % 4]
    sin = np.sin(angle).T[feature % 4] * np.where(feature % 8 < 4, -1.0, 1.0)[:, None]
    row, col = np.arange(128)[:, None], np.arange(128)[None, :]
    earlier = np.broadcast_to((np.arange(8)[None, :] < np.arange(8)[:, None]).reshape(1, 64), (128, 64))
    parts = {"ident": ident, "cos": cos, "sin": sin, "upto": row <= col, "after": row > col,
             "heads16": row // 8 == np.arange(16)[None, :], "heads8": row // 16 == np.arange(8)[None, :],
             "earlier": earlier, "half": np.full((128, NB), -0.5)}
    f32 = np.concatenate([np.asarray(parts[k], np.float32) for k in CONSTS], axis=1)
    causal = np.where(col > row, np.float32(BIG), np.float32(0))
    return f32, np.concatenate([ident, causal], axis=1)


def kernel(**inputs):
    import ml_dtypes
    from concourse import bacc
    from concourse.bass_utils import run_bass_kernel_spmd

    v = {}
    for name, a in inputs.items():
        a = np.asarray(a)
        for layer in ("L0", "L1", "L2", "L3"):
            if name.startswith(layer + "_xattn_"):
                name = layer + "_" + name[len(layer) + 7:]
        v[name] = a
    w, c, r = {}, {}, {}
    for part in ("sa", "ca"):
        for m in "qkvo":
            w[f"L0_{part}_w{m}"] = v[f"L0_{part}_w{m}"]
            if m in "qk":
                w[f"L0_{part}_w{m}r"] = _swap_halves(v[f"L0_{part}_w{m}"])
                c[f"L0_{part}_b{m}r"] = _swap_halves(v[f"L0_{part}_b{m}"])
            if m != "o":
                c[f"L0_{part}_b{m}"] = v[f"L0_{part}_b{m}"]
        r[f"L0_{part}_bo"] = v[f"L0_{part}_bo"]
        for j, m in enumerate("qkv"):
            w[f"L1_{part}_w{m}"] = v[f"L1_{part}_in_w"][j * D:(j + 1) * D].T
            c[f"L1_{part}_b{m}"] = v[f"L1_{part}_in_b"][j * D:(j + 1) * D]
        w[f"L1_{part}_wo"] = v[f"L1_{part}_out_w"].T
        r[f"L1_{part}_bo"] = v[f"L1_{part}_out_b"]
    w["L0_fc1"], w["L0_fc2"] = v["L0_fc1_w"], _blocks(v["L0_fc2_w"], FC)
    w["L1_router"] = v["L1_router_w"].T
    w["L1_fc1"] = v["L1_e_fc1_w"].transpose(2, 0, 1).reshape(D, NE * FF)
    w["L1_fc2"] = v["L1_e_fc2_w"].reshape(NE, D, FC, 128).transpose(3, 0, 2, 1).reshape(128, NE * FF)
    w["L2_in"], w["L2_out"] = v["L2_in_proj_w"], _blocks(v["L2_out_proj_w"], 2)
    for m in "qkvo":
        w[f"L2_w{m}"] = v[f"L2_W{m}"]
        w[f"L3_w{m}"] = v[f"L3_W{m}"].T
        (r if m == "o" else c)[f"L3_b{m}"] = v[f"L3_b{m}"]
    for name in COLS:
        if name not in c and name in v:
            c[name] = v[name]
    c["L1_fc1_b"] = v["L1_e_fc1_b"].reshape(NE * FC, 128).T
    c["L0_fc1_b"] = v["L0_fc1_b"].reshape(FC, 128).T
    c["L2_conv_b"] = v["L2_conv_b"].reshape(4, 128).T
    c["L2_conv_w"] = _blocks(v["L2_conv_w"], 4)
    c["L2_gnorm"] = v["L2_gnorm_w"].reshape(2, 128).T
    r.update(L0_fc2_b=v["L0_fc2_b"], L3_ln_g=v["L3_ln_g"], L3_ln_b=v["L3_ln_b"], L1_router_b=v["L1_router_b"],
             L2_dt_bias=v["L2_dt_bias"], L2_A_log=v["L2_A_log"], L2_D=v["L2_D_skip"])
    consts, consts16 = _constants()
    arrays = {
        "x": v["x"], "ctx_rows": v["ctx_1024"],
        "ctx_cols": v["ctx_1024"].transpose(2, 0, 1).reshape(D, B * LC),
        "mask_pairs": v["mask_BxSxS2_ik1"], "mask_keys": v["mask_1xS2_bf0"],
        "weights": np.concatenate([w[n] for n in WEIGHTS], axis=1),
        "cols": np.concatenate([c[n].reshape(128, -1) for n in COLS], axis=1),
        "rows": np.concatenate([r[n].reshape(1, -1) for n in ROWS], axis=1),
        "expert_b2": v["L1_e_fc2_b"], "consts": consts, "consts16": consts16.astype(ml_dtypes.bfloat16),
    }
    nc = bacc.Bacc("TRN2", target_bir_lowering=False, num_devices=1)
    args = []
    for name, a in arrays.items():
        arrays[name] = a = np.ascontiguousarray(a)
        args.append(nc.dram_tensor(name, a.shape, mybir.dt.from_np(a.dtype), kind="ExternalInput").ap())
    args.append(nc.dram_tensor("out", (B, L, D), F32, kind="ExternalOutput").ap())
    build(nc, *args)
    result = run_bass_kernel_spmd(nc, [arrays], core_ids=[0])
    return result.results[0]["out"]
```

```python
from contextlib import ExitStack

import numpy as np
import concourse.bass as bass
from concourse import mybir

F32 = mybir.dt.float32
BF16 = mybir.dt.bfloat16
I32 = mybir.dt.int32
U8 = mybir.dt.uint8
ALU = mybir.AluOpType
ACT = mybir.ActivationFunctionType
AX = mybir.AxisListType

B, L, LC, D = 64, 128, 77, 128
FF = 512
NE = 8
DI, DS, HM, HP = 256, 128, 4, 64
S, NB = 2, 4
PRESETS = 2
ONE = 16
TURNS = B // (S * NB)
FC = FF // 128
DIN = 2 * DI + 2 * DS + HM
EPS = 1e-5
BIG = -(2.0 ** 60)


class Attention:

    def __init__(self, name, heads, keys, wq, wk, wv, wo, bq=None, bk=None, bv=None, bo=None,
                 rope=False, mask=None, norm=None, kv_norm=None):
        self.name, self.heads, self.keys = name, heads, keys
        self.wq, self.wk, self.wv, self.wo = wq, wk, wv, wo
        self.bq, self.bk, self.bv, self.bo = bq, bk, bv, bo
        self.rope, self.mask, self.norm, self.kv_norm = rope, mask, norm, kv_norm
        self.project = "rope" if rope else "project"
        self.own = keys == L
        self.width = D // heads
        self.halves = heads // 8
        self.quads = heads // 4
        self.scale = self.width ** -0.5


ATT = [
    Attention("L0s", 16, L, "L0_sa_wq", "L0_sa_wk", "L0_sa_wv", "L0_sa_wo", "L0_sa_bq", "L0_sa_bk", "L0_sa_bv",
              "L0_sa_bo", rope=True, mask="causal", norm=0),
    Attention("L0c", 16, LC, "L0_ca_wq", "L0_ca_wk", "L0_ca_wv", "L0_ca_wo", "L0_ca_bq", "L0_ca_bk", "L0_ca_bv",
              "L0_ca_bo", rope=True, norm=1),
    Attention("L1s", 16, L, "L1_sa_wq", "L1_sa_wk", "L1_sa_wv", "L1_sa_wo", "L1_sa_bq", "L1_sa_bk", "L1_sa_bv",
              "L1_sa_bo", norm=3),
    Attention("L1c", 16, LC, "L1_ca_wq", "L1_ca_wk", "L1_ca_wv", "L1_ca_wo", "L1_ca_bq", "L1_ca_bk", "L1_ca_bv",
              "L1_ca_bo", norm=4, kv_norm=5),
    Attention("L2c", 8, LC, "L2_wq", "L2_wk", "L2_wv", "L2_wo", mask="keys", norm=8),
    Attention("L3c", 16, LC, "L3_wq", "L3_wk", "L3_wv", "L3_wo", "L3_bq", "L3_bk", "L3_bv", "L3_bo",
              mask="pairs", norm=9),
]

NORMS = {0: ("L0_ln1_g", "L0_ln1_b"), 1: ("L0_ln2_g", "L0_ln2_b"), 2: ("L0_ln3_g", "L0_ln3_b"),
         3: ("L1_sa_ln_g", "L1_sa_ln_b"), 4: ("L1_ca_q_ln_g", "L1_ca_q_ln_b"),
         5: ("L1_ca_kv_ln_g", "L1_ca_kv_ln_b"), 6: ("L1_moe_ln_g", "L1_moe_ln_b"),
         7: ("L2_m_norm_w", None), 8: ("L2_ca_ln_w", "L2_ca_ln_b"), 9: (None, None), 10: (None, None)}
NORM_KV, NORM_RMS, NORM_NONE, NORM_LAST = 5, 7, 9, 10

WEIGHTS = (["L0_sa_wq", "L0_sa_wqr", "L0_sa_wk", "L0_sa_wkr", "L0_sa_wv", "L0_sa_wo",
            "L0_ca_wq", "L0_ca_wqr", "L0_ca_wk", "L0_ca_wkr", "L0_ca_wv", "L0_ca_wo"]
           + ["L0_fc1", "L0_fc2"]
           + ["L1_sa_wq", "L1_sa_wk", "L1_sa_wv", "L1_sa_wo", "L1_ca_wq", "L1_ca_wk", "L1_ca_wv", "L1_ca_wo",
              "L1_router", "L1_fc1", "L1_fc2"]
           + ["L2_in", "L2_out", "L2_wq", "L2_wk", "L2_wv", "L2_wo", "L3_wq", "L3_wk", "L3_wv", "L3_wo"])
WIDTH = {"L0_fc1": FF, "L0_fc2": FF, "L1_router": NE, "L1_fc1": NE * FF, "L1_fc2": NE * FF, "L2_in": DIN,
         "L2_out": DI}
COLS = ["L0_ln1_g", "L0_ln1_b", "L0_ln2_g", "L0_ln2_b", "L0_ln3_g", "L0_ln3_b", "L0_sa_bq", "L0_sa_bqr",
        "L0_sa_bk", "L0_sa_bkr", "L0_sa_bv", "L0_ca_bq", "L0_ca_bqr", "L0_ca_bk", "L0_ca_bkr", "L0_ca_bv",
        "L1_sa_ln_g", "L1_sa_ln_b", "L1_ca_q_ln_g", "L1_ca_q_ln_b", "L1_ca_kv_ln_g", "L1_ca_kv_ln_b",
        "L1_moe_ln_g", "L1_moe_ln_b", "L1_sa_bq", "L1_sa_bk", "L1_sa_bv", "L1_ca_bq", "L1_ca_bk", "L1_ca_bv",
        "L2_m_norm_w", "L2_ca_ln_w", "L2_ca_ln_b", "L3_bq", "L3_bk", "L3_bv",
        "L0_fc1_b", "L1_fc1_b", "L2_conv_b", "L2_conv_w", "L2_gnorm"]
COL_WIDTH = {"L0_fc1_b": FC, "L1_fc1_b": NE * FC, "L2_conv_b": 4, "L2_conv_w": 16, "L2_gnorm": 2}
ROWS = ["L0_sa_bo", "L0_ca_bo", "L0_fc2_b", "L1_sa_bo", "L1_ca_bo", "L3_bo", "L3_ln_g", "L3_ln_b",
        "L1_router_b", "L2_dt_bias", "L2_A_log", "L2_D"]
ROW_WIDTH = {"L1_router_b": NE, "L2_dt_bias": HM, "L2_A_log": HM, "L2_D": HM}
CONSTS = ["ident", "cos", "sin", "upto", "after", "heads16", "heads8", "earlier", "half"]
CONST_WIDTH = {"heads16": 16, "heads8": 8, "earlier": NE * NE, "half": NB}


def offsets(names, widths, usual=D):
    at, n = {}, 0
    for name in names:
        w = widths.get(name, usual)
        at[name] = (n, w)
        n += w
    return at, n


W_AT, W_N = offsets(WEIGHTS, WIDTH)
W_L1 = W_AT["L1_sa_wq"][0]
C_AT, C_N = offsets(COLS, COL_WIDTH, 1)
R_AT, R_N = offsets(ROWS, ROW_WIDTH)
K_AT, K_N = offsets(CONSTS, CONST_WIDTH)


def norm_steps(n, s):
    return ([("stats", n, s)] if n != NORM_NONE else []) + [("norm", n, s)]


def attention_steps(a, s):
    t = ATT[a]
    keys, values = [(t.project, a, s, "k")], [("values", a, s)]
    queries = norm_steps(t.norm, s) + [(t.project, a, s, "q")]
    if t.own:
        out = norm_steps(t.norm, s) + keys + [(t.project, a, s, "q")] + values
    else:
        out = (norm_steps(t.kv_norm, s) if t.kv_norm is not None else []) + keys + values + queries
    if t.bo:
        out.append(("bias", a, s))
    units = [(b, h) for b in range(NB) for h in range(t.halves)]
    for n in range(len(units) + 2):
        if n < len(units):
            out += [("spread", a, s, *units[n]), ("scores", a, s, *units[n])]
        if 3 <= n and units[n - 3][1] == t.halves - 1:
            out.append(("regroup", a, s, units[n - 3][0]))
        if 2 <= n:
            out.append(("mix", a, s, *units[n - 2]))
        if 1 <= n <= len(units):
            b, h = units[n - 1]
            out += [("turn", a, s, b, 2 * h + q) for q in range(2)]
    return out + [("regroup", a, s, NB - 1), ("turn_out", a, s), ("out", a, s)]


def pass_steps(s):
    out = [("load", s)] + attention_steps(0, s) + attention_steps(1, s)
    out += norm_steps(2, s) + [("bias_mlp", s)] + [("hidden", s, c) for c in range(FC)] + [("mlp", s)]
    out += attention_steps(2, s) + attention_steps(3, s)
    out += norm_steps(6, s) + [("route", s), ("gates", s), ("expert_bias", s)]
    for e in range(NE + 1):
        if e < NE:
            out += [("up", s, e, c) for c in range(FC)]
        if e:
            out.append(("down", s, e - 1))
    out += norm_steps(7, s) + [("step_size", s), ("step_size2", s)]
    out += [("conv", s, 2), ("conv", s, 3), ("decay_in", s, 0), ("decay_in", s, 1)]
    out += [("decay", s, 0), ("decay_in", s, 2), ("decay", s, 1), ("decay_in", s, 3), ("decay", s, 2), ("decay", s, 3)]
    out += [("conv", s, 0), ("pairs", s), ("z", s, 0), ("z", s, 1), ("conv", s, 1)]
    out += [("weigh", s, b) for b in range(NB)] + [("rows", s, h) for h in range(2)]
    out += [("scan", s, h) for h in range(2)] + [("gate_stats", s), ("gate_norm", s)]
    out += [("turn_gate", s, c) for c in range(2)] + [("mamba_out", s)]
    out += attention_steps(4, s) + attention_steps(5, s)
    return out + [("stats", NORM_LAST, s), ("final", s), ("store", s)]


P, V, A, G, Y = "TensorE", "VectorE", "ScalarE", "GpSimd", "SyncE"
PARTS = {
    "load": [(Y, 3.0), (V, 0.3)], "stats": [(V, 1.5), (G, 1.0)], "norm": [(V, 1.1), (P, 0.45), (A, 0.6)],
    "final": [(V, 1.0)], "bias": [(G, 1.2)], "bias_mlp": [(G, 1.2)],
    "project": [(P, 0.85), (A, 0.5)], "rope": [(P, 1.7), (V, 2.2)], "values": [(P, 0.9), (V, 0.6)],
    "spread": [(G, 1.9)], "scores": [(P, 1.71), (V, 2.4), (A, 0.95)],
    "scores masked": [(P, 2.15), (V, 2.4), (A, 0.95)], "scores77 masked": [(P, 1.3), (V, 1.55), (A, 0.61)],
    "project77": [(P, 0.52), (A, 0.35)], "values77": [(P, 0.87), (V, 0.6)],
    "spread77": [(G, 1.2)], "scores77": [(P, 1.03), (V, 1.55), (A, 0.61)],
    "turn": [(P, 0.43), (A, 0.5)], "mix": [(P, 0.6), (A, 0.3)], "regroup": [(P, 0.43), (V, 0.5)],
    "turn_out": [(P, 0.45), (A, 0.6)], "out": [(P, 0.85), (V, 0.7)],
    "hidden": [(P, 0.85), (A, 0.6)], "mlp": [(P, 3.5), (V, 0.65)],
    "route": [(P, 0.1), (V, 0.8), (A, 0.3)], "gates": [(V, 3.1), (P, 0.5), (A, 0.5)], "expert_bias": [(P, 0.87), (V, 0.6)],
    "up": [(P, 0.86), (A, 0.6)], "down": [(P, 3.5), (V, 1.2)],
    "step_size": [(P, 0.1), (V, 0.5), (A, 0.3)], "step_size2": [(V, 2.9)],
    "z": [(P, 0.85), (A, 0.6)], "conv": [(P, 0.85), (V, 3.0), (A, 0.6)], "rows": [(P, 0.43), (V, 1.6)],
    "pairs": [(P, 0.9), (V, 0.7)], "decay_in": [(G, 1.1)], "decay": [(P, 0.85), (A, 0.6)], "weigh": [(G, 1.2)],
    "scan": [(P, 1.7), (V, 0.7), (G, 1.2)], "gate_stats": [(V, 2.4), (G, 1.0)], "gate_norm": [(V, 1.1)],
    "turn_gate": [(P, 0.43), (A, 0.5)], "mamba_out": [(P, 1.7), (V, 0.7)], "store": [(G, 2.4), (Y, 0.1)],
}
TABLE = {"scores": "exp", "route": "exp", "step_size": "exp", "decay": "exp", "up": "gelu", "hidden": "tanh",
         "z": "silu", "conv": "silu"}
SWITCH = 1.3
HOP = 0.8


def parts(step):
    name = step[0]
    if name in ("spread", "scores", "values") and not ATT[step[1]].own:
        name += "77"
    if name.startswith("scores") and ATT[step[1]].mask:
        name += " masked"
    if name == "project" and step[3] == "k" and not ATT[step[1]].own:
        name += "77"
    return PARTS[name]


BY_STREAM = ("load", "final", "bias_mlp", "hidden", "mlp", "route", "gates", "expert_bias", "up", "down", "step_size",
             "step_size2", "z", "conv", "rows", "pairs", "decay_in", "decay", "weigh", "scan", "gate_stats", "gate_norm",
             "turn_gate", "mamba_out", "store")


def stream_of(step):
    return step[1] if step[0] in BY_STREAM else step[2]


SHARED = [(lambda s: ("hidden", s, 0), lambda s: ("mlp", s)), (lambda s: ("route", s), lambda s: ("gates", s)),
          (lambda s: ("up", s, 0, 0), lambda s: ("mamba_out", s))]


def inputs_of(step):
    kind, args = step[0], step[1:]
    if kind in ("project", "rope", "values", "bias", "spread", "scores", "turn", "mix", "regroup", "out"):
        a, s = args[:2]
        t = ATT[a]
        last = (NB - 1, ATT[a - 1].halves - 1)
        units = [(b, h) for b in range(NB) for h in range(t.halves)]
    if kind in ("project", "rope", "values"):
        of = "v" if kind == "values" else args[2]
        if of == "q" or t.own:
            out = [(None, ("norm", t.norm, s), None)]
        elif t.kv_norm is not None:
            out = [(None, ("norm", t.kv_norm, s), None)]
        else:
            out = [(None, ("load", s), Y)]
        if a and of == "k":
            out.append((parts(step)[1][0], ("spread", a - 1, s, *last), None))
        if a and of == "v":
            out.append((V, ("mix", a - 1, s, *last), P))
        return out
    if kind == "bias":
        return [(None, ("norm", t.norm, s), V if t.norm != NORM_NONE else P)]
    if kind == "bias_mlp":
        return [(None, ("norm", 2, args[0]), V)]
    if kind == "norm" and args[0] == NORM_KV:
        return [(None, ("stats", *args), None), (None, ("turn_out", 2, args[1]), P)]
    if kind == "norm" and args[0] == 4:
        return [(None, ("stats", *args), None), (None, ("norm", NORM_KV, args[1]), P), (A, ("values", 3, args[1]), P)]
    if kind == "stats" and args[0] == 4:
        return [(None, ("out", 2, args[1]), None)]
    if kind == "stats" and args[0] in (0, NORM_KV):
        return [(None, ("load", args[1]), Y)]
    if kind == "spread":
        n = units.index(args[2:])
        return ([(None, (t.project, a, s, "k"), None)]
                + ([(None, ("scores", a, s, *units[n - 2]), P)] if n >= 2 else []))
    if kind == "scores":
        n = units.index(args[2:])
        return ([(None, ("spread", *args), None), (None, (t.project, a, s, "q"), None)]
                + ([(V, ("turn", a, s, units[n - 2][0], 2 * units[n - 2][1] + 1), P)] if n >= 2 else []))
    if kind == "turn":
        n = units.index((args[2], args[3] // 2))
        return ([(None, ("scores", a, s, *units[n]), None)]
                + ([(A, ("mix", a, s, *units[n - 1]), P)] if n >= 1 else []))
    if kind == "mix":
        return ([(None, ("turn", *args[:3], 2 * args[3] + q), None) for q in range(2)]
                + [(None, ("values", a, s), None)]
                + ([(A, ("regroup", a, s, args[2] - 1), P)] if args[2] and not args[3] else []))
    if kind == "regroup":
        return [(None, ("mix", *args, t.halves - 1), None)]
    if kind == "out":
        return [(None, ("turn_out", a, s), None)] + ([(V, ("bias", a, s), None)] if t.bo else [])
    s = stream_of(step)
    if kind == "hidden":
        return [(None, ("norm", 2, s), None)]
    if kind == "mlp":
        return [(None, ("hidden", s, FC - 1), None), (V, ("bias_mlp", s), None)]
    if kind == "up":
        e = args[1]
        return [(None, ("norm", 6, s), None)] + ([(A, ("down", s, e - 2), P)] if e >= 2 else [])
    if kind == "expert_bias":
        return [(None, ("gates", s), None)]
    if kind == "down":
        return [(None, ("up", *args, FC - 1), None), (V, ("gates", s), V)]
    if kind in ("z", "conv", "step_size"):
        return [(None, ("norm", 7, s), None)]
    if kind == "step_size2":
        return [(None, ("step_size", s), None)]
    if kind == "rows":
        return [(None, ("conv", s, 1), None), (V, ("step_size2", s), None)]
    if kind == "pairs":
        return [(None, ("conv", s, 3), None)]
    if kind == "decay_in":
        b = args[1]
        return [(None, ("step_size2", s), None)] + ([(None, ("decay", s, b - 2), P)] if b >= 2 else [])
    if kind == "decay":
        return [(None, ("decay_in", *args), None)]
    if kind == "weigh":
        return [(None, ("decay", *args), None), (None, ("pairs", s), None)]
    if kind == "scan":
        return [(None, ("weigh", s, 2 * args[1] + 1), None), (None, ("rows", *args), None), (G, ("z", *args), None)]
    if kind == "gate_stats":
        return [(None, ("scan", s, 1), None)]
    if kind == "turn_gate":
        return [(None, ("gate_norm", s), None)]
    return []


def after(lane, t, length):
    for start, end in lane:
        if start >= t + length:
            break
        t = max(t, end)
    return t


def timetable(streams):
    lanes = {engine: [] for engine in (P, V, A, G, Y)}
    bank_lanes = {b: [] for b in range(8)}
    tables = []
    latest = {}
    begins, ends, banks = {}, {}, {}
    at = [0] * len(streams)
    holder = [None] * len(SHARED)
    freed = [0.0] * len(SHARED)

    def place(n, commit):
        step = streams[n][at[n]]
        waits = [(engine, other, theirs) for engine, other, theirs in inputs_of(step) if other in begins]
        if not inputs_of(step) and at[n]:
            waits = [(None, streams[n][at[n] - 1], None)]
        length_of = parts(step)
        options = banks_of(step) or [()]
        best = None
        for option in options:
            floor = 0.0
            while True:
                t, found = floor, []
                for number, (engine, length) in enumerate(length_of):
                    t = max([t, latest.get((n, engine), 0.0)]
                            + [ends[other, theirs or parts(other)[-1][0]] + HOP for mine, other, theirs in waits
                               if mine == engine or (mine is None and number == 0)])
                    if number == 0:
                        for which, (first, _) in enumerate(SHARED):
                            if first(stream_of(step)) == step:
                                if holder[which] is not None:
                                    return None
                                t = max(t, freed[which] + HOP)
                    t = after(lanes[engine], t, length)
                    if engine == A and step[0] in TABLE:
                        held = max([taken for taken in tables if taken[0] <= t], default=(0.0, None))
                        if held[1] != TABLE[step[0]]:
                            length += SWITCH
                            t = after(lanes[engine], t, length)
                    found.append((engine, t, t + length))
                    t += length + HOP
                if not option:
                    break
                k = next(k for k, (engine, _, _) in enumerate(found) if engine == P)
                lo, hi = found[k][1], found[k + 1][2] + HOP
                clear = max(after(bank_lanes[b], lo, hi - lo) for b in option)
                if clear <= lo:
                    break
                floor = max(floor, clear - (lo - found[0][1]))
            if best is None or found[-1][2] < best[0][-1][2] - 1e-9:
                best = found, option
        found, option = best
        if commit:
            for engine, start, end in found:
                lanes[engine].append((start, end))
                lanes[engine].sort()
                latest[n, engine] = end
                begins.setdefault(step, {})[engine] = start
                ends[step, engine] = end
                if engine == A and step[0] in TABLE:
                    tables.append((start, TABLE[step[0]]))
            if option:
                k = next(k for k, (engine, _, _) in enumerate(found) if engine == P)
                for b in option:
                    bank_lanes[b].append((found[k][1], found[k + 1][2] + HOP))
                    bank_lanes[b].sort()
                banks[step] = option
            for which, (first, final) in enumerate(SHARED):
                if first(stream_of(step)) == step:
                    holder[which] = n
                if final(stream_of(step)) == step:
                    holder[which], freed[which] = None, found[-1][2]
            at[n] += 1
        return found[0][1]

    work = []
    for steps in streams:
        work.append([0.0])
        for step in steps:
            work[-1].append(work[-1][-1] + dict(parts(step)).get(P, 0.0))
    while True:
        starts = {}
        for n in range(len(streams)):
            if at[n] < len(streams[n]):
                start = place(n, False)
                if start is not None:
                    starts[n] = start + LEAD * work[n][at[n]] / work[n][-1] - EAGER.get(streams[n][at[n]][0], 0.0)
        if not starts:
            break
        place(min(starts, key=starts.get), True)
    assert all(at[n] == len(streams[n]) for n in range(len(streams)))
    return begins, banks


LEAD = 10.0
EAGER = {"mamba_out": 8.0, "norm": 4.0, "gates": 8.0, "gate_stats": -4.0, "decay_in": -2.0, "decay": 4.0,
         "step_size2": 2.0, "mlp": -2.0, "rows": 8.0, "final": -4.0, "stats": 8.0, "turn_out": 2.0,
         "z": -1.0, "step_size": 1.0}
CUT = ("stats", 4, 1)


def plans():
    whole, one = pass_steps(0), pass_steps(1)
    cut = one.index(CUT)
    head, tail = one[:cut], one[cut:]
    return [whole, head], [whole, tail + head], [tail]


ANY = [(7,), (6,), (5,), (4,)]
BANKS = {"scores": [(0, 1), (2, 3)], "rope": [(4, 5), (6, 7), (0, 1), (2, 3)], "turn": [(4,), (5,), (6,)]}
WITH_PSUM = ("turn", "mix", "regroup", "norm", "values", "project", "turn_out", "out", "hidden", "mlp", "route", "gates",
             "expert_bias", "up", "down", "step_size", "z", "conv", "rows", "pairs", "decay", "scan", "turn_gate",
             "mamba_out")


def banks_of(step):
    return BANKS.get(step[0]) or (ANY if step[0] in WITH_PSUM else None)


class Plan:

    def __init__(self, streams):
        self.begins, self.banks = timetable(streams)
        self.place = {step: n for steps in streams for n, step in enumerate(steps)}
        self.order = {engine: sorted((step for step in self.begins if engine in self.begins[step]),
                                     key=lambda step: self.begins[step][engine]) for engine in (P, V, A, G, Y)}
        self.ordinal = {}
        for engine, steps in self.order.items():
            count = {}
            for step in steps:
                count[step[0]] = count.get(step[0], 0) + 1
                self.ordinal[engine, step] = count[step[0]]
        self.before, last = {}, {}
        for step in self.order[P]:
            if step in self.banks:
                self.before[step] = list(dict.fromkeys(last[b] for b in self.banks[step] if b in last))
                last.update(dict.fromkeys(self.banks[step], step))

    def precedes(self, other, step):
        if other not in self.place:
            return False
        if stream_of(other) == stream_of(step):
            return self.place[other] <= self.place[step]
        return min(self.begins[other].values()) < min(self.begins[step].values())

    def slot(self, step, depth):
        return self.same(step).index(step) % depth

    def same(self, step):
        found = [other for other in self.place if other[0] == step[0] and other[2] == step[2]]
        return sorted(found, key=self.place.get)

    def earlier(self, step, depth):
        same = self.same(step)
        n = same.index(step) - depth
        return same[n] if n >= 0 else None


def build(nc, x, ctx_rows, ctx_cols, mask_pairs, mask_keys, weights, cols, rows, expert_b2, consts, consts16, out):
    stack = ExitStack()
    with stack:
        def sb(name, shape, dt=F32):
            return stack.enter_context(nc.sbuf_tensor(name, shape, dt))

        sems = {}

        here = [None, None]

        class Signal:

            def __init__(self, name, kind, engine):
                self.sem = stack.enter_context(nc.semaphore(name))
                self.kind, self.engine = kind, engine
                sems[name] = self.sem

            def __call__(self, *other):
                pl, step = here
                other = (self.kind, *other)
                return self.sem, pl.ordinal[self.engine, other] if pl.precedes(other, step) else 0

        w_sb = sb("w_sb", [128, W_N])
        c_sb = sb("c_sb", [128, C_N])
        r_sb = sb("r_sb", [128, R_N])
        k_sb = sb("k_sb", [128, K_N])
        k16 = sb("k16", [128, 2 * 128], BF16)
        b2_sb = sb("b2_sb", [NE, D])
        mk8 = sb("mk8", [128, LC], U8)
        mk16 = sb("mk16", [128, LC], BF16)
        a_neg = sb("a_neg", [128, HM])

        def W(name, a=0, b=None):
            o, n = W_AT[name]
            return w_sb[:, o + a:o + (n if b is None else b)]

        def C(name, j=0):
            o = C_AT[name][0]
            return c_sb[:, o + j:o + j + 1]

        def R(name):
            o, n = R_AT[name]
            return r_sb[:, o:o + n]

        def K(name):
            o, n = K_AT[name]
            return k_sb[:, o:o + n]

        ident = K("ident")
        ident16 = k16[:, 0:128]
        causal16 = k16[:, 128:256]

        xs = [sb(f"x{s}", [128, NB, D]) for s in range(S)]
        xh = [sb(f"xh{s}", [128, NB, D]) for s in range(S)]
        hT = [sb(f"hT{s}", [128, NB * L]) for s in range(S)]
        qT = [sb(f"qT{s}", [128, NB * L]) for s in range(S)]
        kT = [sb(f"kT{s}", [128, NB * L]) for s in range(S)]
        cx = [sb(f"cx{s}", [LC, NB, D]) for s in range(S)]
        cT = [sb(f"cT{s}", [128, NB * LC]) for s in range(S)]
        v1 = [sb(f"v1_{s}", [128, NB * 16, 32]) for s in range(S)]
        mp32 = [sb(f"mp32_{s}", [128, NB, LC], I32) for s in range(S)]
        mp16 = [sb(f"mp16_{s}", [128, NB, LC], BF16) for s in range(S)]
        st = [sb(f"st{s}", [128, NB, 6]) for s in range(S)]
        mv = [sb(f"mv{s}", [128, NB, 2]) for s in range(S)]
        var = [sb(f"var{s}", [128, NB]) for s in range(S)]
        rstd = [sb(f"rstd{s}", [128, NB]) for s in range(S)]
        tmp = sb("tmp", [128, NB * L])
        kx = [sb(f"kx{s}", [128, 2, 8 * L]) for s in range(S)]
        pr = [sb(f"pr{s}", [128, 2, 8 * L]) for s in range(S)]
        pt = [sb(f"pt{s}", [128, 2, 4 * L]) for s in range(S)]
        og = sb("og", [128, 2, 4 * L])
        mx = sb("mx", [128, 2, 8])
        rc = sb("rc", [128, 16])
        hid = sb("hid", [128, FC * NB * L])
        h1 = sb("h1", [128, 2, FC * NB * L])
        lg = sb("lg", [128, NB, NE])
        top = sb("top", [128, NB])
        ex = sb("ex", [128, NB, NE])
        beats, ties = (tmp[:, n * NB * NE * NE:(n + 1) * NB * NE * NE].rearrange("p (b e f) -> p b e f", b=NB, e=NE)
                       for n in range(2))
        rank = sb("rank", [128, NB, NE])
        gates = [sb(f"gates{s}", [128, NB, NE]) for s in range(S)]
        gT = [sb(f"gT{s}", [NE, NB * L]) for s in range(S)]
        dt_u = sb("dt_u", [128, NB * HM])
        dt_e = sb("dt_e", [128, NB * HM])
        dt_z = sb("dt_z", [128, NB * HM])
        dt_z2 = sb("dt_z2", [128, NB * HM])
        dt_p = sb("dt_p", [128, NB * HM])
        dtv = sb("dtv", [128, NB, HM])
        dta = sb("dta", [128, NB, HM])
        gm = sb("gm", [128, NB, L])
        m1a = sb("m1a", [128, 2, HM * L])
        lw = sb("lw", [128, NB, HM * L])
        ch = h1[:, 0, :].rearrange("p (c t) -> p c t", c=4)
        zg = h1[:, 1, 0:NB * DI].rearrange("p (b i) -> p b i", b=NB)
        uT = h1[:, 1, 0:2 * NB * L].rearrange("p (c t) -> p c t", c=2)
        dbx = sb("dbx", [128, NB, DI])
        yg = sb("yg", [128, NB, DI])

        ps = stack.enter_context(nc.psum_tensor("ps", [128, 8, 512], F32))

        loads = [stack.enter_context(nc.semaphore(f"loads{s}")) for s in range(S)]
        preset_link = stack.enter_context(nc.semaphore("preset_link"))
        preset = stack.enter_context(nc.semaphore("preset"))
        fetched = stack.enter_context(nc.semaphore("fetched"))
        fetched_rest = stack.enter_context(nc.semaphore("fetched_rest"))
        stores = [stack.enter_context(nc.semaphore(f"stores{s}")) for s in range(S)]
        arrived = stack.enter_context(nc.semaphore("arrived"))
        cleared = stack.enter_context(nc.semaphore("cleared"))
        go = stack.enter_context(nc.semaphore("go"))
        begun = stack.enter_context(nc.semaphore("begun"))
        dve_link = stack.enter_context(nc.semaphore("dve_link"))
        pool_link = stack.enter_context(nc.semaphore("pool_link"))
        sems.update(dve_link=dve_link, pool_link=pool_link)
        mask_ready = Signal("mask_ready", "load", V)
        variance = Signal("variance", "stats", V)
        rstd_ready = Signal("rstd_ready", "stats", G)
        normed = Signal("normed", "norm", V)
        norm_turned = Signal("norm_turned", "norm", P)
        hT_ready = Signal("hT_ready", "norm", A)
        final_normed = Signal("final_normed", "final", V)
        out_rows = Signal("out_rows", "store", G)
        projected = Signal("projected", "project", P)
        proj_ready = Signal("proj_ready", "project", A)
        rope_made = Signal("rope_made", "rope", P)
        rope_ready = Signal("rope_ready", "rope", V)
        values_made = Signal("values_made", "values", P)
        values_ready = Signal("values_ready", "values", V)
        bias_added = Signal("bias_added", "bias", G)
        keys_spread = Signal("keys_spread", "spread", G)
        scores_made = Signal("scores_made", "scores", P)
        scores_shifted = Signal("scores_shifted", "scores", V)
        probs_ready = Signal("probs_ready", "scores", A)
        probs_turned = Signal("probs_turned", "turn", P)
        probsT_ready = Signal("probsT_ready", "turn", A)
        mixed = Signal("mixed", "mix", P)
        gathered = Signal("gathered", "mix", A)
        regrouped = Signal("regrouped", "regroup", P)
        heads_ready = Signal("heads_ready", "regroup", V)
        out_turned = Signal("out_turned", "turn_out", P)
        outT_ready = Signal("outT_ready", "turn_out", A)
        out_made = Signal("out_made", "out", P)
        x_updated = Signal("x_updated", "out", V)
        mlp_biased = Signal("mlp_biased", "bias_mlp", G)
        hidden_made = Signal("hidden_made", "hidden", P)
        hidden_ready = Signal("hidden_ready", "hidden", A)
        mlp_made = Signal("mlp_made", "mlp", P)
        mlp_added = Signal("mlp_added", "mlp", V)
        logits_made = Signal("logits_made", "route", P)
        logits_ready = Signal("logits_ready", "route", V)
        route_exp = Signal("route_exp", "route", A)
        gates_ready = Signal("gates_ready", "gates", V)
        gates_turned = Signal("gates_turned", "gates", P)
        gT_ready = Signal("gT_ready", "gates", A)
        expert_bias_made = Signal("expert_bias_made", "expert_bias", P)
        expert_bias_added = Signal("expert_bias_added", "expert_bias", V)
        up_made = Signal("up_made", "up", P)
        up_ready = Signal("up_ready", "up", A)
        down_made = Signal("down_made", "down", P)
        down_added = Signal("down_added", "down", V)
        dt_made = Signal("dt_made", "step_size", P)
        dt_abs = Signal("dt_abs", "step_size", V)
        dt_exp = Signal("dt_exp", "step_size", A)
        dt_ready = Signal("dt_ready", "step_size2", V)
        z_made = Signal("z_made", "z", P)
        z_ready = Signal("z_ready", "z", A)
        conv_in = Signal("conv_in", "conv", P)
        conv_done = Signal("conv_done", "conv", V)
        conv_ready = Signal("conv_ready", "conv", A)
        rows_made = Signal("rows_made", "rows", P)
        rows_scaled = Signal("rows_scaled", "rows", V)
        pairs_made = Signal("pairs_made", "pairs", P)
        pairs_ready = Signal("pairs_ready", "pairs", V)
        decay_in = Signal("decay_in", "decay_in", G)
        decay_sums = Signal("decay_sums", "decay", P)
        decay_exp = Signal("decay_exp", "decay", A)
        decay_ready = Signal("decay_ready", "weigh", G)
        scan_made = Signal("scan_made", "scan", P)
        scan_added = Signal("scan_added", "scan", V)
        scan_gated = Signal("scan_gated", "scan", G)
        gate_var = Signal("gate_var", "gate_stats", V)
        gate_rstd = Signal("gate_rstd", "gate_stats", G)
        gate_normed = Signal("gate_normed", "gate_norm", V)
        gate_turned = Signal("gate_turned", "turn_gate", P)
        uT_ready = Signal("uT_ready", "turn_gate", A)
        mamba_made = Signal("mamba_made", "mamba_out", P)
        mamba_added = Signal("mamba_added", "mamba_out", V)

        RELEASED = {"scores": scores_shifted, "turn": probsT_ready, "mix": gathered, "regroup": heads_ready,
                    "norm": hT_ready, "project": proj_ready, "rope": rope_ready, "values": values_ready, "turn_out": outT_ready,
                    "out": x_updated, "hidden": hidden_ready, "mlp": mlp_added, "route": logits_ready,
                    "gates": gT_ready, "expert_bias": expert_bias_added, "up": up_ready, "down": down_added,
                    "step_size": dt_abs, "z": z_ready, "conv": conv_done, "rows": rows_scaled,
                    "pairs": pairs_ready, "decay": decay_exp, "scan": scan_added, "turn_gate": uT_ready,
                    "mamba_out": mamba_added}

        def bank(pl, step, n=0):
            return ps[:, pl.banks[step][n], :]

        def of_attention(a):
            return ATT[a], ATT[a].keys

        def source(n, s):
            return (cx[s], LC) if n == NORM_KV else (xs[s], L)

        class Link:

            def __init__(self, eng, sem):
                self.eng, self.sem, self.n = eng, sem, 0

            def __call__(self, ins):
                self.n += 1
                ins.then_inc(self.sem, 1)
                self.eng.wait_ge(self.sem, self.n)

        def now(pl, step):
            here[:] = [pl, step]

        def loaded(s):
            pl, step = here
            return loads[s], 4 * 16 if pl.precedes(("load", s), step) else 0

        def tell(eng, ins, signal, *own):
            assert (signal.kind, *own) == here[1]
            ins.then_inc(signal.sem, 1)
            eng.wait_ge(*signal(*own))

        def turn_begin(eng, it, share):
            eng.drain().then_inc(arrived, 1)
            eng.wait_ge(go, 2 * it - 1)
            eng.sem_inc(begun, 1)
            for sem in list(sems.values())[share::5]:
                eng.sem_clear(sem)
            eng.sem_inc(arrived, 1)
            eng.wait_ge(go, 2 * it)
            eng.sem_inc(begun, 1)

        def all_turns(eng, turn):
            turn(FIRST, 0)
            with eng.Fori(1, TURNS) as it:
                turn(LOOP, it)
            turn(LAST, TURNS)

        FIRST, LOOP, LAST = (Plan(streams) for streams in plans())
        block = stack.enter_context(nc.Block())

        @block.sync
        def _(sp):
            def load(s, it):
                g = it * (S * NB) + s * NB
                sp.dma_start(xs[s][:], x[bass.ds(g, NB)].rearrange("b q d -> q b d")).then_inc(loads[s], 16)
                sp.dma_start(cx[s][:], ctx_rows[bass.ds(g, NB)].rearrange("b q d -> q b d")).then_inc(loads[s], 16)
                sp.dma_start(cT[s][:], ctx_cols[:, bass.ds(g * LC, NB * LC)]).then_inc(loads[s], 16)
                sp.dma_start(mp32[s][:], mask_pairs[bass.ds(g, NB)].rearrange("b q k -> q b k")).then_inc(loads[s], 16)

            sp.dma_start(k_sb[:], consts).then_inc(fetched, 16)
            sp.dma_start(k16[:], consts16).then_inc(fetched, 16)
            sp.dma_start(c_sb[:], cols).then_inc(fetched, 16)
            sp.dma_start(r_sb[:], rows.broadcast_to([128, R_N])).then_inc(fetched, 16)
            load(0, 0)
            sp.dma_start(w_sb[:, 0:W_L1], weights[:, 0:W_L1]).then_inc(fetched, 16)
            sp.dma_start(mk8[:], mask_keys.broadcast_to([128, LC])).then_inc(fetched, 16)
            sp.dma_start(b2_sb[:], expert_b2).then_inc(fetched, 16)

            def turn(pl, it):
                if pl is not FIRST:
                    sp.wait_ge(arrived, it * 8 - 4)
                    sp.sem_inc(cleared, 1)
                    sp.sem_inc(go, 1)
                    for s in range(S):
                        sp.sem_clear(loads[s])
                    if ("load", 0) in pl.place:
                        load(0, it)
                    for sem in list(sems.values())[4::5]:
                        sp.sem_clear(sem)
                    sp.wait_ge(arrived, it * 8)
                    sp.sem_inc(cleared, 1)
                    sp.sem_inc(go, 1)
                for step in pl.order[Y]:
                    now(pl, step)
                    kind, s = step
                    if kind == "load" and s:
                        sp.wait_ge(*final_normed(s))
                        load(s, it)
                        if pl is FIRST:
                            sp.dma_start(w_sb[:, W_L1:W_N], weights[:, W_L1:W_N]).then_inc(fetched_rest, 16)
                    elif kind == "store":
                        sp.wait_ge(*out_rows(s))
                        g = it * (S * NB) - s * NB
                        sp.dma_start(out[bass.ds(g, NB)].rearrange("b q d -> q b d"), xh[s][:]).then_inc(stores[s], 16)
            all_turns(sp, turn)
            for s in range(S):
                sp.wait_ge(stores[s], TURNS * 16)

        @block.tensor
        def _(pe):
            pe.wait_ge(fetched, 16 * 7)
            pe.wait_ge(preset, PRESETS)
            mm = nc.tensor.matmul
            tr = nc.tensor.transpose

            def turn(pl, it):
                if pl is not FIRST:
                    turn_begin(pe, it, 0)
                for step in pl.order[P]:
                    now(pl, step)
                    kind, args = step[0], step[1:]
                    for old in pl.before[step]:
                        released = RELEASED[old[0]]
                        pe.wait_ge(released.sem, pl.ordinal[released.engine, old])
                    p = bank(pl, step)
                    if kind == "norm":
                        n, s = args
                        _, m = source(n, s)
                        if n == NORM_NONE:
                            pe.wait_ge(*x_updated(4, s))
                        else:
                            pe.wait_ge(*normed(n, s))
                        rows_ = xs[s] if n == NORM_NONE else xh[s]
                        for b in range(NB):
                            i = tr(p[:, b * m:(b + 1) * m], rows_[0:m, b, :], ident[0:m, 0:m])
                        i.then_inc(norm_turned.sem, 1)
                    elif kind in ("project", "rope"):
                        a, s, what = args
                        t, keys = of_attention(a)
                        src, n = hT[s], NB * L
                        if what == "k" and not t.own:
                            n = NB * LC
                            if t.kv_norm is None:
                                src = cT[s]
                                pe.wait_ge(*loaded(s))
                        if what == "q" or t.own or t.kv_norm is not None:
                            pe.wait_ge(*hT_ready(t.norm if what == "q" or t.own else t.kv_norm, s))
                        if pl is FIRST and a == 2:
                            pe.wait_ge(fetched_rest, 16)
                        w = t.wq if what == "q" else t.wk
                        i = mm(p[:, 0:n], W(w), src[:, 0:n], start=True, stop=True)
                        if t.rope:
                            i = mm(bank(pl, step, 1)[:, 0:n], W(w + "r"), src[:, 0:n], start=True, stop=True)
                        i.then_inc((rope_made if t.rope else projected).sem, 1)
                    elif kind == "values":
                        a, s = args
                        t, keys = of_attention(a)
                        src = cT[s] if not t.own and t.kv_norm is None else hT[s]
                        for b in range(NB):
                            i = mm(p[0:keys, b * D:(b + 1) * D], src[:, b * keys:(b + 1) * keys], W(t.wv),
                                   start=True, stop=True)
                        i.then_inc(values_made.sem, 1)
                    elif kind == "scores":
                        a, s, b, h = args
                        t, keys = of_attention(a)
                        pe.wait_ge(*keys_spread(a, s, b, h))
                        first = b == 0 and h == 0
                        if first:
                            pe.wait_ge(*(rope_ready if t.rope else proj_ready)(a, s, "q"))
                        mask = {"causal": causal16, "keys": mk16[:], "pairs": mp16[s][:, b, :], None: None}[t.mask]
                        if first and t.mask == "pairs":
                            pe.wait_ge(*mask_ready(s))
                        k = kx[s][:, pl.slot(step, 2), :]
                        for j in range(2):
                            o = bank(pl, step, j)[:, 0:4 * keys]
                            i = mm(o, qT[s][:, b * L:(b + 1) * L], k[:, 4 * j * keys:4 * (j + 1) * keys],
                                   start=True, stop=mask is None)
                            if mask is not None:
                                i = mm(o.rearrange("p (h k) -> p h k", h=4), ident16,
                                       mask.unsqueeze(1).broadcast_to([128, 4, keys]), start=False, stop=True)
                        i.then_inc(scores_made.sem, 1)
                    elif kind == "turn":
                        a, s, b, q = args
                        t, keys = of_attention(a)
                        unit = ("scores", a, s, b, q // 2)
                        pe.wait_ge(*probs_ready(*unit[1:]))
                        for j in range(4):
                            c = (4 * (q % 2) + j) * keys
                            i = tr(p[0:keys, j * L:(j + 1) * L], pr[s][:, pl.slot(unit, 2), c:c + keys], ident)
                        i.then_inc(probs_turned.sem, 1)
                    elif kind == "mix":
                        a, s, b, h = args
                        t, keys = of_attention(a)
                        if b == 0 and h == 0:
                            pe.wait_ge(*values_ready(a, s))
                        for q in range(2):
                            pe.wait_ge(*probsT_ready(a, s, b, 2 * h + q))
                            for j in range(4):
                                i = mm(ps[32 * j:32 * j + 32, pl.banks[step][0], q * L:(q + 1) * L],
                                       v1[s][0:keys, b * t.heads + 8 * h + 4 * q + j, :],
                                       pt[s][0:keys, q, j * L:(j + 1) * L], start=True, stop=True)
                        i.then_inc(mixed.sem, 1)
                    elif kind == "regroup":
                        a, s, b = args
                        t, keys = of_attention(a)
                        pe.wait_ge(*gathered(a, s, b, t.halves - 1))
                        for q in range(t.quads):
                            i = tr(p[:, q * L:(q + 1) * L], og[:, s, q * L:(q + 1) * L], ident)
                        i.then_inc(regrouped.sem, 1)
                    elif kind == "turn_out":
                        a, s = args
                        pe.wait_ge(*heads_ready(a, s, NB - 1))
                        for b in range(NB):
                            i = tr(p[:, b * L:(b + 1) * L], xh[s][:, b, :], ident)
                        i.then_inc(out_turned.sem, 1)
                    elif kind == "out":
                        a, s = args
                        pe.wait_ge(*outT_ready(a, s))
                        for b in range(NB):
                            i = mm(p[:, b * D:(b + 1) * D], hT[s][:, b * L:(b + 1) * L], W(ATT[a].wo), start=True, stop=True)
                        i.then_inc(out_made.sem, 1)
                    elif kind == "hidden":
                        s, c = args
                        pe.wait_ge(*hT_ready(2, s))
                        mm(p, W("L0_fc1", c * 128, (c + 1) * 128), hT[s][:], start=True, stop=True)\
                            .then_inc(hidden_made.sem, 1)
                    elif kind == "mlp":
                        (s,) = args
                        pe.wait_ge(*hidden_ready(s, FC - 1))
                        for b in range(NB):
                            for c in range(FC):
                                i = mm(p[:, b * D:(b + 1) * D], hid[:, c * NB * L + b * L:c * NB * L + (b + 1) * L],
                                       W("L0_fc2", c * D, (c + 1) * D), start=c == 0, stop=c == FC - 1)
                        i.then_inc(mlp_made.sem, 1)
                    elif kind == "route":
                        (s,) = args
                        pe.wait_ge(*hT_ready(6, s))
                        for b in range(NB):
                            i = mm(p[:, b * NE:(b + 1) * NE], hT[s][:, b * L:(b + 1) * L], W("L1_router"), start=True, stop=True)
                        i.then_inc(logits_made.sem, 1)
                    elif kind == "gates":
                        (s,) = args
                        pe.wait_ge(*gates_ready(s))
                        for b in range(NB):
                            i = tr(p[0:NE, b * L:(b + 1) * L], gates[s][:, b, :], ident)
                        i.then_inc(gates_turned.sem, 1)
                    elif kind == "expert_bias":
                        (s,) = args
                        pe.wait_ge(*gT_ready(s))
                        for b in range(NB):
                            i = mm(p[:, b * D:(b + 1) * D], gT[s][:, b * L:(b + 1) * L], b2_sb[:], start=True, stop=True)
                        i.then_inc(expert_bias_made.sem, 1)
                    elif kind == "up":
                        s, e, c = args
                        mm(p, W("L1_fc1", e * FF + c * 128, e * FF + (c + 1) * 128), hT[s][:], start=True, stop=True)\
                            .then_inc(up_made.sem, 1)
                    elif kind == "down":
                        s, e = args
                        pe.wait_ge(*up_ready(s, e, FC - 1))
                        for b in range(NB):
                            for c in range(FC):
                                i = mm(p[:, b * D:(b + 1) * D], h1[:, e % 2, c * NB * L + b * L:c * NB * L + (b + 1) * L],
                                       W("L1_fc2", e * FF + c * D, e * FF + (c + 1) * D), start=c == 0, stop=c == FC - 1)
                        i.then_inc(down_made.sem, 1)
                    elif kind == "step_size":
                        (s,) = args
                        pe.wait_ge(*hT_ready(7, s))
                        for b in range(NB):
                            i = mm(p[:, b * HM:(b + 1) * HM], hT[s][:, b * L:(b + 1) * L], W("L2_in", DIN - HM, DIN),
                                   start=True, stop=True)
                        i.then_inc(dt_made.sem, 1)
                    elif kind == "z":
                        s, h = args
                        for j in range(2):
                            b = 2 * h + j
                            i = mm(p[:, j * DI:(j + 1) * DI], hT[s][:, b * L:(b + 1) * L], W("L2_in", 0, DI), start=True, stop=True)
                        i.then_inc(z_made.sem, 1)
                    elif kind == "conv":
                        s, c = args
                        mm(p, W("L2_in", DI + c * 128, DI + (c + 1) * 128), hT[s][:], start=True, stop=True)\
                            .then_inc(conv_in.sem, 1)
                    elif kind == "rows":
                        s, h = args
                        pe.wait_ge(*conv_ready(s, 1))
                        for j in range(2):
                            for c in range(2):
                                i = tr(p[:, j * DI + c * 128:j * DI + (c + 1) * 128],
                                       ch[:, c, (2 * h + j) * L:(2 * h + j + 1) * L], ident)
                        i.then_inc(rows_made.sem, 1)
                    elif kind == "pairs":
                        (s,) = args
                        pe.wait_ge(*conv_ready(s, 3))
                        for b in range(NB):
                            i = mm(p[:, b * L:(b + 1) * L], ch[:, 2, b * L:(b + 1) * L], ch[:, 3, b * L:(b + 1) * L],
                                   start=True, stop=True)
                        i.then_inc(pairs_made.sem, 1)
                    elif kind == "decay":
                        s, b = args
                        pe.wait_ge(*decay_in(s, b))
                        mm(p, K("after"), m1a[:, b % 2, :], start=True, stop=True).then_inc(decay_sums.sem, 1)
                    elif kind == "scan":
                        s, h = args
                        pe.wait_ge(*decay_ready(s, 2 * h + 1))
                        pe.wait_ge(*rows_scaled(s, h))
                        for j in range(2):
                            b = 2 * h + j
                            for g in range(HM):
                                i = mm(p[:, j * DI + g * HP:j * DI + (g + 1) * HP], lw[:, b, g * L:(g + 1) * L],
                                       dbx[:, b, g * HP:(g + 1) * HP], start=True, stop=True)
                        i.then_inc(scan_made.sem, 1)
                    elif kind == "turn_gate":
                        s, c = args
                        pe.wait_ge(*gate_normed(s))
                        for b in range(NB):
                            i = tr(p[:, b * L:(b + 1) * L], yg[:, b, c * 128:(c + 1) * 128], ident)
                        i.then_inc(gate_turned.sem, 1)
                    elif kind == "mamba_out":
                        (s,) = args
                        pe.wait_ge(*uT_ready(s, 1))
                        for b in range(NB):
                            for c in range(2):
                                i = mm(p[:, b * D:(b + 1) * D], uT[:, c, b * L:(b + 1) * L], W("L2_out", c * D, (c + 1) * D),
                                       start=c == 0, stop=c == 1)
                        i.then_inc(mamba_made.sem, 1)
                    else:
                        raise AssertionError(kind)

            all_turns(pe, turn)

        @block.scalar
        def _(act):
            act.wait_ge(fetched, 16 * 7)
            nc.scalar.activation(a_neg[:], R("L2_A_log"), ACT.Exp).then_inc(preset, 1)
            act.wait_ge(preset, PRESETS)
            go_act = nc.scalar.activation

            def turn(pl, it):
                if pl is not FIRST:
                    turn_begin(act, it, 1)
                for step in pl.order[A]:
                    now(pl, step)
                    kind, args = step[0], step[1:]
                    p = bank(pl, step) if step in pl.banks else None
                    if kind == "norm":
                        n, s = args
                        _, m = source(n, s)
                        gain, bias = NORMS[n]
                        act.wait_ge(*norm_turned(n, s))
                        o, i = hT[s][:, 0:NB * m], p[:, 0:NB * m]
                        if gain is None:
                            go_act(o, i, ACT.Copy).then_inc(hT_ready.sem, 1)
                        elif bias is None:
                            go_act(o, i, ACT.Copy, scale=C(gain)).then_inc(hT_ready.sem, 1)
                        else:
                            go_act(o, i, ACT.Identity, scale=C(gain), bias=C(bias)).then_inc(hT_ready.sem, 1)
                    elif kind == "project":
                        a, s, what = args
                        t, keys = of_attention(a)
                        n = NB * (L if what == "q" else keys)
                        dst = (qT if what == "q" else kT)[s]
                        act.wait_ge(*projected(*args))
                        bias = t.bq if what == "q" else t.bk
                        if what == "k" and a:
                            act.wait_ge(*keys_spread(a - 1, s, NB - 1, ATT[a - 1].halves - 1))
                        if bias:
                            go_act(dst[:, 0:n], p[:, 0:n], ACT.Identity, bias=C(bias)).then_inc(proj_ready.sem, 1)
                        else:
                            go_act(dst[:, 0:n], p[:, 0:n], ACT.Copy).then_inc(proj_ready.sem, 1)
                    elif kind == "scores":
                        a, s, b, h = args
                        t, keys = of_attention(a)
                        act.wait_ge(*scores_shifted(*args))
                        v = pr[s][:, pl.slot(step, 2), 0:8 * keys]
                        go_act(v, v, ACT.Exp, scale=t.scale).then_inc(probs_ready.sem, 1)
                    elif kind == "turn":
                        a, s, b, q = args
                        t, keys = of_attention(a)
                        old = pl.earlier(("mix", a, s, b, q // 2), 1)
                        if old:
                            act.wait_ge(*mixed(*old[1:]))
                        act.wait_ge(*probs_turned(*args))
                        go_act(pt[s][0:keys, q % 2, :], p[0:keys, :], ACT.Copy).then_inc(probsT_ready.sem, 1)
                    elif kind == "mix":
                        a, s, b, h = args
                        t, keys = of_attention(a)
                        act.wait_ge(*mixed(*args))
                        if b and not h:
                            act.wait_ge(*regrouped(a, s, b - 1))
                        elif a and not h:
                            act.wait_ge(*regrouped(a - 1, s, NB - 1))
                        go_act(og[:, s, 2 * h * L:2 * (h + 1) * L], p[:, 0:2 * L], ACT.Copy)\
                            .then_inc(gathered.sem, 1)
                    elif kind == "turn_out":
                        a, s = args
                        bias = ATT[a].bv
                        act.wait_ge(*out_turned(a, s))
                        act.wait_ge(*values_made(a, s))
                        if bias:
                            go_act(hT[s][:], p, ACT.Identity, bias=C(bias)).then_inc(outT_ready.sem, 1)
                        else:
                            go_act(hT[s][:], p, ACT.Copy).then_inc(outT_ready.sem, 1)
                    elif kind == "hidden":
                        s, c = args
                        if c == 0:
                            act.wait_ge(*mlp_made(1 - s))
                        act.wait_ge(*hidden_made(s, c))
                        go_act(hid[:, c * NB * L:(c + 1) * NB * L], p, ACT.Gelu_apprx_tanh, bias=C("L0_fc1_b", c))\
                            .then_inc(hidden_ready.sem, 1)
                    elif kind == "route":
                        (s,) = args
                        act.wait_ge(*logits_ready(s))
                        go_act(ex[:], lg[:], ACT.Exp).then_inc(route_exp.sem, 1)
                    elif kind == "gates":
                        (s,) = args
                        act.wait_ge(*gates_turned(s))
                        go_act(gT[s][:], p[0:NE, :], ACT.Copy).then_inc(gT_ready.sem, 1)
                    elif kind == "up":
                        s, e, c = args
                        if e == 0 and c == 0:
                            act.wait_ge(*down_made(1 - s, NE - 2))
                            act.wait_ge(*rows_made(1 - s, 1))
                            act.wait_ge(*pairs_made(1 - s))
                        if e == 1 and c == 0:
                            act.wait_ge(*down_made(1 - s, NE - 1))
                            act.wait_ge(*mamba_made(1 - s))
                        act.wait_ge(*up_made(s, e, c))
                        go_act(h1[:, e % 2, c * NB * L:(c + 1) * NB * L], p, ACT.Gelu, bias=C("L1_fc1_b", e * FC + c))\
                            .then_inc(up_ready.sem, 1)
                    elif kind == "step_size":
                        (s,) = args
                        act.wait_ge(*dt_abs(s))
                        go_act(dt_e[:], dt_e[:], ACT.Exp, scale=-1.0).then_inc(dt_exp.sem, 1)
                    elif kind == "z":
                        s, h = args
                        if h == 0:
                            act.wait_ge(*down_made(1 - s, NE - 1))
                            act.wait_ge(*mamba_made(1 - s))
                        act.wait_ge(*z_made(s, h))
                        go_act(zg[:, 2 * h:2 * h + 2, :], p, ACT.Silu).then_inc(z_ready.sem, 1)
                    elif kind == "conv":
                        s, c = args
                        act.wait_ge(*conv_done(s, c))
                        go_act(ch[:, c, :], ch[:, c, :], ACT.Silu).then_inc(conv_ready.sem, 1)
                    elif kind == "decay":
                        s, b = args
                        act.wait_ge(*decay_sums(s, b))
                        go_act(lw[:, b, :], p, ACT.Exp).then_inc(decay_exp.sem, 1)
                    elif kind == "turn_gate":
                        s, c = args
                        act.wait_ge(*gate_turned(s, c))
                        go_act(uT[:, c, :], p, ACT.Copy, scale=C("L2_gnorm", c)).then_inc(uT_ready.sem, 1)

            all_turns(act, turn)

        @block.vector
        def _(dve):
            link = Link(dve, preset_link)
            for t in v1:
                link(nc.vector.memset(t[:], 0.0))
                link(nc.vector.memset(t[:, :, ONE:ONE + 1], 1.0))
            dve.wait_ge(fetched, 16 * 7)
            nc.vector.tensor_scalar(mk16[:], mk8[:], 0.0, BIG, ALU.not_equal, ALU.mult).then_inc(preset, 1)
            dve.wait_ge(preset, PRESETS)
            link = Link(dve, dve_link)
            v_ = nc.vector

            def turn(pl, it):
                if pl is not FIRST:
                    turn_begin(dve, it, 2)
                link.n = 0
                for step in pl.order[V]:
                    now(pl, step)
                    kind, args = step[0], step[1:]
                    p = bank(pl, step) if step in pl.banks else None
                    if kind == "load":
                        (s,) = args
                        dve.wait_ge(*loaded(s))
                        tell(dve, v_.tensor_scalar(mp16[s][:], mp32[s][:], 0.0, BIG, ALU.is_equal, ALU.mult), mask_ready, s)
                    elif kind == "stats":
                        n, s = args
                        src, m = source(n, s)
                        if n in (0, NORM_KV):
                            dve.wait_ge(*loaded(s))
                        for b in range(NB):
                            i = v_.bn_stats(st[s][0:m, b, :], src[0:m, b, :])
                        link(i)
                        for b in range(NB):
                            i = v_.bn_aggr(mv[s][0:m, b, :], st[s][0:m, b, :])
                        link(i)
                        if n == NORM_RMS:
                            link(v_.tensor_tensor(var[s][:], mv[s][:, :, 0], mv[s][:, :, 0], ALU.mult))
                            link(v_.tensor_tensor(var[s][:], var[s][:], mv[s][:, :, 1], ALU.add))
                            tell(dve, v_.tensor_scalar(var[s][:], var[s][:], EPS, None, ALU.add), variance, n, s)
                        else:
                            tell(dve, v_.tensor_scalar(var[s][0:m], mv[s][0:m, :, 1], EPS, None, ALU.add), variance, n, s)
                    elif kind == "final":
                        (s,) = args
                        dve.wait_ge(*rstd_ready(NORM_LAST, s))
                        for b in range(NB):
                            i = v_.tensor_scalar(xh[s][:, b, :], xs[s][:, b, :], mv[s][:, b, 0:1], rstd[s][:, b:b + 1],
                                                 ALU.subtract, ALU.mult)
                        tell(dve, i, final_normed, s)
                    elif kind == "norm":
                        n, s = args
                        if n == NORM_NONE:
                            tell(dve, v_.tensor_copy(rc[:, 0:1], mx[:, 0, 0:1]), normed, n, s)
                            continue
                        src, m = source(n, s)
                        dve.wait_ge(*rstd_ready(n, s))
                        if n == 0 and pl is not FIRST:
                            dve.wait_ge(stores[s], it * 16)
                        if n == NORM_KV:
                            dve.wait_ge(*out_turned(2, s))
                        if n == 4:
                            dve.wait_ge(*norm_turned(NORM_KV, s))
                        for b in range(NB):
                            if n == NORM_RMS:
                                i = v_.tensor_scalar(xh[s][:, b, :], src[:, b, :], rstd[s][:, b:b + 1], None, ALU.mult)
                            else:
                                i = v_.tensor_scalar(xh[s][0:m, b, :], src[0:m, b, :], mv[s][0:m, b, 0:1],
                                                     rstd[s][0:m, b:b + 1], ALU.subtract, ALU.mult)
                        tell(dve, i, normed, n, s)
                    elif kind == "rope":
                        a, s, what = args
                        t, keys = of_attention(a)
                        m = L if what == "q" else keys
                        dst = (qT if what == "q" else kT)[s]
                        if what == "k" and a:
                            dve.wait_ge(*keys_spread(a - 1, s, NB - 1, ATT[a - 1].halves - 1))
                        dve.wait_ge(*rope_made(*args))
                        bias = t.bq if what == "q" else t.bk

                        def by_batch(ap):
                            return ap[:, 0:NB * m].rearrange("p (b t) -> p b t", b=NB)

                        def table(name):
                            return K(name)[:, 0:m].unsqueeze(1).broadcast_to([128, NB, m])
                        link(v_.scalar_tensor_tensor(by_batch(dst[:]), by_batch(p), C(bias), table("cos"), ALU.add, ALU.mult))
                        link(v_.scalar_tensor_tensor(by_batch(tmp[:]), by_batch(bank(pl, step, 1)), C(bias + "r"), table("sin"),
                                                     ALU.add, ALU.mult))
                        tell(dve, v_.tensor_tensor(dst[:, 0:NB * m], dst[:, 0:NB * m], tmp[:, 0:NB * m], ALU.add),
                             rope_ready, *args)
                    elif kind == "values":
                        a, s = args
                        t, keys = of_attention(a)
                        dve.wait_ge(*values_made(a, s))
                        tell(dve, v_.tensor_copy(v1[s][0:keys, 0:NB * t.heads, 0:t.width],
                                                 p[0:keys, :].rearrange("p (n d) -> p n d", d=t.width)), values_ready, a, s)
                    elif kind == "scores":
                        a, s, b, h = args
                        t, keys = of_attention(a)
                        dve.wait_ge(*scores_made(*args))
                        m = mx[:, s, :]
                        lo = pl.banks[step][0]
                        tile = ps[:, lo:lo + 2, 0:4 * keys].rearrange("p c (h k) -> p c h k", h=4)
                        link(v_.tensor_reduce(m, tile, AX.X, ALU.max, negate=True))
                        old = pl.earlier(step, 2)
                        if old:
                            for q in range(2):
                                dve.wait_ge(*probs_turned(*old[1:4], 2 * old[4] + q))
                        dst = pr[s][:, pl.slot(step, 2), 0:8 * keys].rearrange("p (c h k) -> p c h k", c=2, h=4)
                        tell(dve, v_.tensor_tensor(
                            dst, tile, m.rearrange("p (c h) -> p c h", c=2).unsqueeze(3).broadcast_to([128, 2, 4, keys]),
                            ALU.add), scores_shifted, *args)
                    elif kind == "regroup":
                        a, s, b = args
                        t, keys = of_attention(a)
                        dve.wait_ge(*regrouped(a, s, b))
                        tile = p[:, 0:t.heads * 32].rearrange("p (h w) -> p h w", w=32)
                        link(v_.reciprocal(rc[:, 0:t.heads], tile[:, :, ONE]))
                        tell(dve, v_.tensor_tensor(xh[s][:, b, :].rearrange("p (h w) -> p h w", w=t.width),
                                                   tile[:, :, 0:t.width],
                                                   rc[:, 0:t.heads].unsqueeze(2).broadcast_to([128, t.heads, t.width]),
                                                   ALU.mult), heads_ready, a, s, b)
                    elif kind in ("out", "mlp", "expert_bias", "mamba_out"):
                        s = args[-1]
                        made, added = {"out": (out_made, x_updated), "mlp": (mlp_made, mlp_added),
                                       "expert_bias": (expert_bias_made, expert_bias_added),
                                       "mamba_out": (mamba_made, mamba_added)}[kind]
                        dve.wait_ge(*made(*args))
                        if kind == "out" and ATT[args[0]].bo:
                            dve.wait_ge(*bias_added(*args))
                        if kind == "mlp":
                            dve.wait_ge(*mlp_biased(s))
                        flat = xs[s][:].rearrange("p b d -> p (b d)")
                        tell(dve, v_.tensor_tensor(flat, p, flat, ALU.add), added, *args)
                    elif kind == "route":
                        (s,) = args
                        dve.wait_ge(*logits_made(s))
                        link(v_.tensor_tensor(lg[:], p[:, 0:NB * NE].rearrange("p (b e) -> p b e", b=NB),
                                              R("L1_router_b").unsqueeze(1).broadcast_to([128, NB, NE]), ALU.add))
                        link(v_.tensor_reduce(top[:], lg[:], AX.X, ALU.max))
                        tell(dve, v_.tensor_tensor(lg[:], lg[:], top[:].unsqueeze(2).broadcast_to([128, NB, NE]),
                                                   ALU.subtract), logits_ready, s)
                    elif kind == "gates":
                        (s,) = args
                        rows_ = lg[:].unsqueeze(2).broadcast_to([128, NB, NE, NE])
                        cols_ = lg[:].unsqueeze(3).broadcast_to([128, NB, NE, NE])
                        link(v_.tensor_tensor(beats, rows_, cols_, ALU.is_gt))
                        link(v_.tensor_tensor(ties, rows_, cols_, ALU.is_equal))
                        link(v_.tensor_tensor(ties.rearrange("p b e f -> p b (e f)"), ties.rearrange("p b e f -> p b (e f)"),
                                              K("earlier").unsqueeze(1).broadcast_to([128, NB, NE * NE]), ALU.mult))
                        link(v_.tensor_tensor(beats, beats, ties, ALU.add))
                        link(v_.tensor_reduce(rank[:], beats, AX.X, ALU.add))
                        dve.wait_ge(*route_exp(s))
                        link(v_.scalar_tensor_tensor(rank[:], rank[:], 1.5, ex[:], ALU.is_lt, ALU.mult))
                        link(v_.tensor_reduce(top[:], rank[:], AX.X, ALU.add))
                        link(v_.reciprocal(top[:], top[:]))
                        tell(dve, v_.tensor_tensor(gates[s][:], rank[:], top[:].unsqueeze(2).broadcast_to([128, NB, NE]),
                                                   ALU.mult), gates_ready, s)
                    elif kind == "down":
                        s, e = args
                        dve.wait_ge(*down_made(s, e))
                        for b in range(NB):
                            i = v_.scalar_tensor_tensor(xs[s][:, b, :], p[:, b * D:(b + 1) * D], gates[s][:, b, e:e + 1],
                                                        xs[s][:, b, :], ALU.mult, ALU.add)
                        tell(dve, i, down_added, s, e)
                    elif kind == "step_size":
                        (s,) = args
                        dve.wait_ge(*dt_made(s))
                        link(v_.tensor_tensor(dt_u[:].rearrange("p (b h) -> p b h", b=NB),
                                              p[:, 0:NB * HM].rearrange("p (b h) -> p b h", b=NB),
                                              R("L2_dt_bias").unsqueeze(1).broadcast_to([128, NB, HM]), ALU.add))
                        tell(dve, v_.scalar_tensor_tensor(dt_e[:], dt_u[:], -1.0, dt_u[:], ALU.mult, ALU.max), dt_abs, s)
                    elif kind == "step_size2":
                        (s,) = args
                        dve.wait_ge(*dt_exp(s))
                        link(v_.tensor_scalar(dt_z[:], dt_e[:], 2.0, None, ALU.add))
                        link(v_.reciprocal(dt_z[:], dt_z[:]))
                        link(v_.tensor_tensor(dt_z[:], dt_z[:], dt_e[:], ALU.mult))
                        link(v_.tensor_tensor(dt_z2[:], dt_z[:], dt_z[:], ALU.mult))
                        link(v_.tensor_scalar(dt_p[:], dt_z2[:], 1.0 / 13, None, ALU.mult))
                        for c in (11, 9, 7, 5, 3):
                            link(v_.scalar_tensor_tensor(dt_p[:], dt_p[:], 1.0 / c, dt_z2[:], ALU.add, ALU.mult))
                        link(v_.scalar_tensor_tensor(dt_p[:], dt_p[:], 1.0, dt_z[:], ALU.add, ALU.mult))
                        link(v_.tensor_scalar(dt_u[:], dt_u[:], 0.0, None, ALU.max))
                        flat = dtv[:].rearrange("p b h -> p (b h)")
                        link(v_.scalar_tensor_tensor(flat, dt_p[:], 2.0, dt_u[:], ALU.mult, ALU.add))
                        tell(dve, v_.scalar_tensor_tensor(dta[:], dtv[:], -1.0, a_neg[:].unsqueeze(1).broadcast_to([128, NB, HM]),
                                                          ALU.mult, ALU.mult), dt_ready, s)
                    elif kind == "conv":
                        s, c = args
                        if c == 0:
                            dve.wait_ge(*down_made(1 - s, NE - 2))
                            dve.wait_ge(*rows_made(1 - s, 1))
                            dve.wait_ge(*pairs_made(1 - s))
                        dve.wait_ge(*conv_in(s, c))
                        taps = [C("L2_conv_w", 4 * c + j) for j in range(4)]
                        src = p.rearrange("p (b t) -> p b t", b=NB)
                        dst = ch[:, c, :].rearrange("p (b t) -> p b t", b=NB)
                        link(v_.tensor_scalar(ch[:, c, :], p, taps[3], C("L2_conv_b", c), ALU.mult, ALU.add))
                        for j in (1, 2, 3):
                            i = v_.scalar_tensor_tensor(dst[:, :, j:L], src[:, :, 0:L - j], taps[3 - j], dst[:, :, j:L],
                                                        ALU.mult, ALU.add)
                            if j < 3:
                                link(i)
                        tell(dve, i, conv_done, s, c)
                    elif kind == "rows":
                        s, h = args
                        dve.wait_ge(*rows_made(s, h))
                        for j in range(2):
                            b = 2 * h + j
                            v = p[:, j * DI:(j + 1) * DI].rearrange("p (h w) -> p h w", h=HM)
                            v_.tensor_tensor(dbx[:, b, :].rearrange("p (h w) -> p h w", h=HM), v,
                                                  dtv[:, b, :].unsqueeze(2).broadcast_to([128, HM, HP]), ALU.mult)
                            i = v_.tensor_tensor(yg[:, b, :].rearrange("p (h w) -> p h w", h=HM), v,
                                                 R("L2_D").unsqueeze(2).broadcast_to([128, HM, HP]), ALU.mult)
                        tell(dve, i, rows_scaled, s, h)
                    elif kind == "pairs":
                        (s,) = args
                        dve.wait_ge(*pairs_made(s))
                        tell(dve, v_.tensor_tensor(gm[:], p.rearrange("p (b t) -> p b t", b=NB),
                                                   K("upto").unsqueeze(1).broadcast_to([128, NB, L]), ALU.mult),
                             pairs_ready, s)
                    elif kind == "scan":
                        s, h = args
                        dve.wait_ge(*scan_made(s, h))
                        tell(dve, v_.tensor_tensor(yg[:, 2 * h:2 * h + 2, :].rearrange("p b i -> p (b i)"), p,
                                                   yg[:, 2 * h:2 * h + 2, :].rearrange("p b i -> p (b i)"), ALU.add),
                             scan_added, s, h)
                    elif kind == "gate_stats":
                        (s,) = args
                        dve.wait_ge(*scan_gated(s, 1))
                        for b in range(NB):
                            i = v_.bn_stats(st[s][:, b, :], yg[:, b, :])
                        link(i)
                        for b in range(NB):
                            i = v_.bn_aggr(mv[s][:, b, :], st[s][:, b, :])
                        link(i)
                        link(v_.tensor_tensor(var[s][:], mv[s][:, :, 0], mv[s][:, :, 0], ALU.mult))
                        link(v_.tensor_tensor(var[s][:], var[s][:], mv[s][:, :, 1], ALU.add))
                        tell(dve, v_.tensor_scalar(var[s][:], var[s][:], EPS, None, ALU.add), gate_var, s)
                    elif kind == "gate_norm":
                        (s,) = args
                        dve.wait_ge(*gate_rstd(s))
                        for b in range(NB):
                            i = v_.tensor_scalar(yg[:, b, :], yg[:, b, :], rstd[s][:, b:b + 1], None, ALU.mult)
                        tell(dve, i, gate_normed, s)

            all_turns(dve, turn)

        @block.gpsimd
        def _(pool):
            pool.wait_ge(fetched, 16 * 7)
            pool.wait_ge(preset, PRESETS)
            link = Link(pool, pool_link)
            g_ = nc.gpsimd

            def turn(pl, it):
                if pl is not FIRST:
                    turn_begin(pool, it, 3)
                link.n = 0
                for step in pl.order[G]:
                    now(pl, step)
                    kind, args = step[0], step[1:]
                    if kind == "stats":
                        n, s = args
                        _, m = source(n, s)
                        pool.wait_ge(*variance(n, s))
                        tell(pool, g_.tensor_tensor(rstd[s][0:m], var[s][0:m], K("half")[0:m], ALU.pow), rstd_ready, n, s)
                    elif kind == "gate_stats":
                        (s,) = args
                        pool.wait_ge(*gate_var(s))
                        tell(pool, g_.tensor_tensor(rstd[s][:], var[s][:], K("half"), ALU.pow), gate_rstd, s)
                    elif kind in ("bias", "bias_mlp"):
                        s = args[-1]
                        n = ATT[args[0]].norm if kind == "bias" else 2
                        row = ATT[args[0]].bo if kind == "bias" else "L0_fc2_b"
                        if n == NORM_NONE:
                            pool.wait_ge(*norm_turned(n, s))
                        else:
                            pool.wait_ge(*normed(n, s))
                        tell(pool, g_.tensor_tensor(xs[s][:], xs[s][:], R(row).unsqueeze(1).broadcast_to([128, NB, D]),
                                                    ALU.add), bias_added if kind == "bias" else mlp_biased, *args)
                    elif kind == "spread":
                        a, s, b, h = args
                        t, keys = of_attention(a)
                        if b == 0 and h == 0:
                            pool.wait_ge(*(rope_ready if t.rope else proj_ready)(a, s, "k"))
                        old = pl.earlier(step, 2)
                        if old:
                            pool.wait_ge(*scores_made(*old[1:]))
                        dst = kx[s][:, pl.slot(step, 2), 0:8 * keys].rearrange("p (h k) -> p h k", h=8)
                        masks = K("heads16")[:, 8 * h:8 * h + 8] if t.heads == 16 else K("heads8")
                        tell(pool, g_.tensor_tensor(
                            dst, kT[s][:, b * keys:(b + 1) * keys].unsqueeze(1).broadcast_to([128, 8, keys]),
                            masks.unsqueeze(2).broadcast_to([128, 8, keys]), ALU.mult), keys_spread, *args)
                    elif kind == "decay_in":
                        s, b = args
                        pool.wait_ge(*dt_ready(s))
                        if b >= 2:
                            pool.wait_ge(*decay_sums(s, b - 2))
                        tell(pool, g_.tensor_tensor(m1a[:, b % 2, :].rearrange("p (h t) -> p h t", h=HM),
                                              K("upto").unsqueeze(1).broadcast_to([128, HM, L]),
                                              dta[:, b, :].unsqueeze(2).broadcast_to([128, HM, L]), ALU.mult),
                             decay_in, s, b)
                    elif kind == "weigh":
                        s, b = args
                        pool.wait_ge(*decay_exp(s, b))
                        pool.wait_ge(*pairs_ready(s))
                        v = lw[:, b, :].rearrange("p (h t) -> p h t", h=HM)
                        tell(pool, g_.tensor_tensor(v, v, gm[:, b, :].unsqueeze(1).broadcast_to([128, HM, L]), ALU.mult),
                             decay_ready, s, b)
                    elif kind == "scan":
                        s, h = args
                        pool.wait_ge(*scan_added(s, h))
                        pool.wait_ge(*z_ready(s, h))
                        v = yg[:, 2 * h:2 * h + 2, :]
                        tell(pool, g_.tensor_tensor(v, v, zg[:, 2 * h:2 * h + 2, :], ALU.mult), scan_gated, s, h)
                    elif kind == "store":
                        (s,) = args
                        pool.wait_ge(*final_normed(s))
                        link(g_.tensor_tensor(xh[s][:], xh[s][:], R("L3_ln_g").unsqueeze(1).broadcast_to([128, NB, D]), ALU.mult))
                        tell(pool, g_.tensor_tensor(xh[s][:], xh[s][:], R("L3_ln_b").unsqueeze(1).broadcast_to([128, NB, D]),
                                                    ALU.add), out_rows, s)

            all_turns(pool, turn)


def _swap_halves(a):
    return a.reshape(*a.shape[:-1], 16, 2, 4)[..., ::-1, :].reshape(a.shape)


def _blocks(a, n):
    return a.reshape(n, 128, -1).transpose(1, 0, 2).reshape(128, -1)


def _constants():
    ident = np.eye(128, dtype=np.float32)
    inverse = np.float32(1.0) / np.float32(10000.0) ** (np.arange(0, 8, 2, dtype=np.float32) / np.float32(8))
    angle = np.outer(np.arange(128, dtype=np.float32), inverse.astype(np.float32)).astype(np.float32)
    feature = np.arange(128)
    cos = np.cos(angle).T[feature % 4]
    sin = np.sin(angle).T[feature % 4] * np.where(feature % 8 < 4, -1.0, 1.0)[:, None]
    row, col = np.arange(128)[:, None], np.arange(128)[None, :]
    earlier = np.broadcast_to((np.arange(8)[None, :] < np.arange(8)[:, None]).reshape(1, 64), (128, 64))
    parts = {"ident": ident, "cos": cos, "sin": sin, "upto": row <= col, "after": row > col,
             "heads16": row // 8 == np.arange(16)[None, :], "heads8": row // 16 == np.arange(8)[None, :],
             "earlier": earlier, "half": np.full((128, NB), -0.5)}
    f32 = np.concatenate([np.asarray(parts[k], np.float32) for k in CONSTS], axis=1)
    causal = np.where(col > row, np.float32(BIG), np.float32(0))
    return f32, np.concatenate([ident, causal], axis=1)


def kernel(**inputs):
    import ml_dtypes
    from concourse import bacc
    from concourse.bass_utils import run_bass_kernel_spmd

    v = {}
    for name, a in inputs.items():
        a = np.asarray(a)
        for layer in ("L0", "L1", "L2", "L3"):
            if name.startswith(layer + "_xattn_"):
                name = layer + "_" + name[len(layer) + 7:]
        v[name] = a
    w, c, r = {}, {}, {}
    for part in ("sa", "ca"):
        for m in "qkvo":
            w[f"L0_{part}_w{m}"] = v[f"L0_{part}_w{m}"]
            if m in "qk":
                w[f"L0_{part}_w{m}r"] = _swap_halves(v[f"L0_{part}_w{m}"])
                c[f"L0_{part}_b{m}r"] = _swap_halves(v[f"L0_{part}_b{m}"])
            if m != "o":
                c[f"L0_{part}_b{m}"] = v[f"L0_{part}_b{m}"]
        r[f"L0_{part}_bo"] = v[f"L0_{part}_bo"]
        for j, m in enumerate("qkv"):
            w[f"L1_{part}_w{m}"] = v[f"L1_{part}_in_w"][j * D:(j + 1) * D].T
            c[f"L1_{part}_b{m}"] = v[f"L1_{part}_in_b"][j * D:(j + 1) * D]
        w[f"L1_{part}_wo"] = v[f"L1_{part}_out_w"].T
        r[f"L1_{part}_bo"] = v[f"L1_{part}_out_b"]
    w["L0_fc1"], w["L0_fc2"] = v["L0_fc1_w"], _blocks(v["L0_fc2_w"], FC)
    w["L1_router"] = v["L1_router_w"].T
    w["L1_fc1"] = v["L1_e_fc1_w"].transpose(2, 0, 1).reshape(D, NE * FF)
    w["L1_fc2"] = v["L1_e_fc2_w"].reshape(NE, D, FC, 128).transpose(3, 0, 2, 1).reshape(128, NE * FF)
    w["L2_in"], w["L2_out"] = v["L2_in_proj_w"], _blocks(v["L2_out_proj_w"], 2)
    for m in "qkvo":
        w[f"L2_w{m}"] = v[f"L2_W{m}"]
        w[f"L3_w{m}"] = v[f"L3_W{m}"].T
        (r if m == "o" else c)[f"L3_b{m}"] = v[f"L3_b{m}"]
    for name in COLS:
        if name not in c and name in v:
            c[name] = v[name]
    c["L1_fc1_b"] = v["L1_e_fc1_b"].reshape(NE * FC, 128).T
    c["L0_fc1_b"] = v["L0_fc1_b"].reshape(FC, 128).T
    c["L2_conv_b"] = v["L2_conv_b"].reshape(4, 128).T
    c["L2_conv_w"] = _blocks(v["L2_conv_w"], 4)
    c["L2_gnorm"] = v["L2_gnorm_w"].reshape(2, 128).T
    r.update(L0_fc2_b=v["L0_fc2_b"], L3_ln_g=v["L3_ln_g"], L3_ln_b=v["L3_ln_b"], L1_router_b=v["L1_router_b"],
             L2_dt_bias=v["L2_dt_bias"], L2_A_log=v["L2_A_log"], L2_D=v["L2_D_skip"])
    consts, consts16 = _constants()
    arrays = {
        "x": v["x"], "ctx_rows": v["ctx_1024"],
        "ctx_cols": v["ctx_1024"].transpose(2, 0, 1).reshape(D, B * LC),
        "mask_pairs": v["mask_BxSxS2_ik1"], "mask_keys": v["mask_1xS2_bf0"],
        "weights": np.concatenate([w[n] for n in WEIGHTS], axis=1),
        "cols": np.concatenate([c[n].reshape(128, -1) for n in COLS], axis=1),
        "rows": np.concatenate([r[n].reshape(1, -1) for n in ROWS], axis=1),
        "expert_b2": v["L1_e_fc2_b"], "consts": consts, "consts16": consts16.astype(ml_dtypes.bfloat16),
    }
    nc = bacc.Bacc("TRN2", target_bir_lowering=False, num_devices=1)
    args = []
    for name, a in arrays.items():
        arrays[name] = a = np.ascontiguousarray(a)
        args.append(nc.dram_tensor(name, a.shape, mybir.dt.from_np(a.dtype), kind="ExternalInput").ap())
    args.append(nc.dram_tensor("out", (B, L, D), F32, kind="ExternalOutput").ap())
    build(nc, *args)
    result = run_bass_kernel_spmd(nc, [arrays], core_ids=[0])
    return result.results[0]["out"]
```
